# Optimizing a Trainium2 kernel written in Bass

```python
import numpy as np
import jax
import jax.numpy as jnp

def _softmax(x, axis=-1):
    return jax.nn.softmax(x, axis=axis)

def _gelu(x):
    return jax.nn.gelu(x, approximate=True)

def _silu(x):
    return jax.nn.silu(x)

def _sigmoid(x):
    return jax.nn.sigmoid(x)

def _layernorm(x, axis=-1, eps=1e-05):
    m = jnp.mean(x, axis=axis, keepdims=True)
    v = jnp.var(x, axis=axis, keepdims=True)
    return (x - m) / jnp.sqrt(v + eps)

def _scatter_add(tgt, idx, src, axis=0):
    return tgt.at[idx].add(src)

def _segment_sum(src, seg, n):
    return jax.ops.segment_sum(src, seg, n)
kernel_name = 'mk_decoder_preln_d1_seqx_r4_83931d'

def setup_inputs(seed: int=0):
    np.random.seed(seed)
    _w = jnp.asarray

    def _rec_inputs():
        import jax
        import jax.numpy as jnp
        _rk = jax.random.key(seed)
        x = 7.22e-05 + 1 * jax.random.normal(jax.random.fold_in(_rk, 1), (8, 112, 256), jnp.float32)
        _lenS = 112 - jax.random.randint(jax.random.fold_in(_rk, 7), (8,), 0, max(1, 112 // 4) + 1, jnp.int32)
        _lenS2 = 375 - jax.random.randint(jax.random.fold_in(_rk, 8), (8,), 0, max(1, 375 // 4) + 1, jnp.int32)
        _ctx_1024P = jax.random.normal(jax.random.fold_in(_rk, 11), (8, 16, 256), jnp.float32)
        _ctx_1024c = jax.random.dirichlet(jax.random.fold_in(_rk, 511), 0.3 * jnp.ones((16,), jnp.float32), (8, 375))
        _ctx_1024t = jnp.einsum('bsk,bkd->bsd', _ctx_1024c, _ctx_1024P)
        _ctx_1024t = _ctx_1024t * jax.lax.rsqrt(jnp.mean(jnp.square(_ctx_1024t)) + 1e-12) * 0.953939
        ctx_1024 = 4.13588e-05 + 0.999923 * (_ctx_1024t + 0.3 * jax.random.normal(jax.random.fold_in(_rk, 611), (8, 375, 256), jnp.float32))
        _validS = jnp.arange(112)[None, :] < _lenS[:, None]
        _validS2 = jnp.arange(375)[None, :] < _lenS2[:, None]
        _causal = jnp.tril(jnp.ones((112, 112), dtype=bool))
        mask_SxS2_ik0 = jnp.where(jnp.broadcast_to(_validS2[0:1, :], (112, 375)), 0, 1).astype(jnp.int32)
        return (x, ctx_1024, mask_SxS2_ik0)
    x, ctx_1024, mask_SxS2_ik0 = _rec_inputs()

    def _L0_attn_setup():
        import jax, jax.numpy as jnp
        import numpy as np
        NUM_HEADS = 16
        STRIDE = 32
        WINDOW = 64

        def _sparse_mask(n: int) -> jnp.ndarray:
            i = jnp.arange(n)[:, None]
            j = jnp.arange(n)[None, :]
            return (j % STRIDE == 0) | (jnp.abs(i - j) <= WINDOW)
        key = jax.random.key(seed)
        k0, k1, k2 = jax.random.split(key, 3)
        d = 256
        return {'x': jax.random.normal(k0, (1, 512, d), dtype=jnp.float32), 'w_qkv': jax.random.normal(k1, (d, 3 * d), dtype=jnp.float32) / np.sqrt(d), 'b_qkv': jnp.zeros((3 * d,), dtype=jnp.float32), 'w_out': jax.random.normal(k2, (d, d), dtype=jnp.float32) / np.sqrt(d), 'b_out': jnp.zeros((d,), dtype=jnp.float32)}
    _L0_attn_all = _L0_attn_setup()
    _L0_attn_in = {k: v for k, v in _L0_attn_all.items() if k in ('w_qkv', 'b_qkv', 'w_out', 'b_out')}
    del _L0_attn_all

    def _L0_xattn_setup():
        import jax, jax.numpy as jnp
        import numpy as np
        import math
        N, S, T, D = (4, 512, 512, 256)
        key = jax.random.key(seed)
        ks = jax.random.split(key, 6)
        scale = 1.0 / math.sqrt(D)
        return {'query': jax.random.normal(ks[0], (N, S, D), dtype=jnp.float32), 'key': jax.random.normal(ks[1], (N, T, D), dtype=jnp.float32), 'value': jax.random.normal(ks[2], (N, T, D), dtype=jnp.float32), 'attn_mask': jnp.tril(jnp.ones((S, T), dtype=jnp.int32)), 'Wq': jax.random.normal(ks[3], (D, D), dtype=jnp.float32) * scale, 'Wk': jax.random.normal(ks[4], (D, D), dtype=jnp.float32) * scale, 'Wv': jax.random.normal(ks[5], (D, D), dtype=jnp.float32) * scale}
    _L0_xattn_all = _L0_xattn_setup()
    _L0_xattn_in = {k: v for k, v in _L0_xattn_all.items() if k in ('Wq', 'Wk', 'Wv')}
    del _L0_xattn_all

    def _L0_ffn_setup():
        import jax, jax.numpy as jnp
        import numpy as np
        EMB = 256
        FF = 4 * EMB

        def _ternary(w):
            scale = jnp.maximum(jnp.mean(jnp.abs(w)), 1e-08)
            w_t = jnp.clip(jnp.round(w / scale), -1.0, 1.0)
            return w + jax.lax.stop_gradient(w_t - w)
        key = jax.random.key(seed)
        kx, k1, k2, kb1, kb2 = jax.random.split(key, 5)
        x = jax.random.normal(kx, (4, 512, EMB), dtype=jnp.float32)
        lim1 = 1.0 / np.sqrt(EMB)
        lim2 = 1.0 / np.sqrt(FF)
        W1 = jax.random.uniform(k1, (FF, EMB), jnp.float32, -lim1, lim1)
        b1 = jax.random.uniform(kb1, (FF,), jnp.float32, -lim1, lim1)
        W2 = jax.random.uniform(k2, (EMB, FF), jnp.float32, -lim2, lim2)
        b2 = jax.random.uniform(kb2, (EMB,), jnp.float32, -lim2, lim2)
        return {'x': x, 'W1': W1, 'b1': b1, 'W2': W2, 'b2': b2}
    _L0_ffn_all = _L0_ffn_setup()
    _L0_ffn_in = {k: v for k, v in _L0_ffn_all.items() if k in ('W1', 'b1', 'W2', 'b2')}
    del _L0_ffn_all
    return {'x': x, 'ctx_1024': ctx_1024, 'mask_SxS2_ik0': mask_SxS2_ik0, 'L0_attn_w_qkv': _L0_attn_in['w_qkv'], 'L0_attn_b_qkv': _L0_attn_in['b_qkv'], 'L0_attn_w_out': _L0_attn_in['w_out'], 'L0_attn_b_out': _L0_attn_in['b_out'], 'L0_xattn_Wq': _L0_xattn_in['Wq'], 'L0_xattn_Wk': _L0_xattn_in['Wk'], 'L0_xattn_Wv': _L0_xattn_in['Wv'], 'L0_ffn_W1': _L0_ffn_in['W1'], 'L0_ffn_b1': _L0_ffn_in['b1'], 'L0_ffn_W2': _L0_ffn_in['W2'], 'L0_ffn_b2': _L0_ffn_in['b2']}

def reference(x, ctx_1024, mask_SxS2_ik0, L0_attn_w_qkv, L0_attn_b_qkv, L0_attn_w_out, L0_attn_b_out, L0_xattn_Wq, L0_xattn_Wk, L0_xattn_Wv, L0_ffn_W1, L0_ffn_b1, L0_ffn_W2, L0_ffn_b2):
    import jax
    import jax.numpy as jnp

    def _L0_attn_ref(x, w_qkv, b_qkv, w_out, b_out):
        import jax, jax.numpy as jnp
        import numpy as np
        NUM_HEADS = 16
        STRIDE = 32
        WINDOW = 64

        def _sparse_mask(n: int) -> jnp.ndarray:
            i = jnp.arange(n)[:, None]
            j = jnp.arange(n)[None, :]
            return (j % STRIDE == 0) | (jnp.abs(i - j) <= WINDOW)
        b, n, d = x.shape
        h = NUM_HEADS
        dh = d // h
        scale = dh ** (-0.5)
        qkv = x @ w_qkv + b_qkv
        q, k, v = jnp.split(qkv, 3, axis=-1)
        q = q.reshape(b, n, h, dh).transpose(0, 2, 1, 3)
        k = k.reshape(b, n, h, dh).transpose(0, 2, 1, 3)
        v = v.reshape(b, n, h, dh).transpose(0, 2, 1, 3)
        scores = jnp.einsum('bhid,bhjd->bhij', q, k) * scale
        mask = _sparse_mask(n)
        scores = jnp.where(mask, scores, -jnp.inf)
        attn = jax.nn.softmax(scores, axis=-1)
        out = jnp.einsum('bhij,bhjd->bhid', attn, v)
        out = out.transpose(0, 2, 1, 3).reshape(b, n, d)
        return out @ w_out + b_out

    def _L0_xattn_ref(query, key, value, attn_mask, Wq, Wk, Wv):
        import jax, jax.numpy as jnp
        import numpy as np
        import math
        N, S, T, D = (4, 512, 512, 256)
        q = jnp.einsum('nsd,ed->nse', query, Wq)
        k = jnp.einsum('ntd,ed->nte', key, Wk)
        v = jnp.einsum('ntd,ed->nte', value, Wv)
        dot = jnp.einsum('nse,nte->nst', q, k) / jnp.sqrt(jnp.asarray(D, q.dtype))
        dot = jnp.where(attn_mask == 0, -jnp.inf, dot)
        scores = jax.nn.softmax(dot, axis=-1)
        y = jnp.einsum('nst,nte->nse', scores, v)
        return y

    def _L0_ffn_ref(x, W1, b1, W2, b2):
        import jax, jax.numpy as jnp
        import numpy as np
        EMB = 256
        FF = 4 * EMB

        def _ternary(w):
            scale = jnp.maximum(jnp.mean(jnp.abs(w)), 1e-08)
            w_t = jnp.clip(jnp.round(w / scale), -1.0, 1.0)
            return w + jax.lax.stop_gradient(w_t - w)
        h = jnp.einsum('bsd,fd->bsf', x, _ternary(W1)) + b1
        h = jax.nn.gelu(h, approximate=False)
        out = jnp.einsum('bsf,df->bsd', h, _ternary(W2)) + b2
        return out
    x = x + _L0_attn_ref(_layernorm(x, axis=-1), L0_attn_w_qkv, L0_attn_b_qkv, L0_attn_w_out, L0_attn_b_out)
    x = x + _L0_xattn_ref(_layernorm(x, axis=-1), ctx_1024, ctx_1024, mask_SxS2_ik0, L0_xattn_Wq, L0_xattn_Wk, L0_xattn_Wv)
    x = x + _L0_ffn_ref(_layernorm(x, axis=-1), L0_ffn_W1, L0_ffn_b1, L0_ffn_W2, L0_ffn_b2)
    return x

_drawn_inputs = setup_inputs


def setup_inputs(seed=0):
    import zlib

    import numpy as np

    out = dict(_drawn_inputs(seed))
    spreads = {'L0_attn_b_qkv': (0.0, 0.1), 'L0_attn_b_out': (0.0, 0.1)}
    factors = {'L0_ffn_b1': 25.597, 'L0_ffn_b2': 64.0}
    for name, (base, spread) in spreads.items():
        noise = np.random.default_rng([zlib.crc32(name.encode()), seed]).standard_normal(out[name].shape)
        drawn = base * np.exp(spread * noise) if base else spread * noise
        out[name] = jnp.asarray(drawn.astype(out[name].dtype))
    for name, factor in factors.items():
        out[name] = (out[name] * factor).astype(out[name].dtype)
    return out
```

```python
from contextlib import ExitStack

import concourse.bass as bass
from concourse import mybir

ALU = mybir.AluOpType
ACT = mybir.ActivationFunctionType
AX = mybir.AxisListType
F32 = mybir.dt.float32
F32R = mybir.dt.float32r
BF16 = mybir.dt.bfloat16
I32 = mybir.dt.int32

B, S, D = 8, 112, 256
T = B * S
P = 128
KD = D // P
NH, DH = 16, 16
S2 = 375
CC, CP = 3, 125
F = 1024
FB = F // P
TC = 512
HALVES = 2
HB = B // HALVES
HT = HB * S
NG, GH = 4, 4
STRIDE, WINDOW = 32, 64
EPS = 1e-5
BIG = -1.0e30
PARTS = 3
QK = 6 * DH
QKM = QK + 2
Q_RUNS = [(0, 0, 3), (3, 0, 2), (5, 0, 1)]
K_RUNS = [(b, p, 1) for b, p in enumerate((0, 0, 0, 1, 1, 2))]


def build(nc, x, ctx_rows, ctx_cols, mask, w_qkv, b_qk, b_v, w_out, b_out, wq, wk, wv_t,
          w1_t, b1, w2_t, b2, eye, eye_b, k_ones, band, band_t, out):
    with ExitStack() as stack:
        def sb(name, shape, dt=F32, where=stack):
            return where.enter_context(nc.sbuf_tensor(name, shape, dt))

        def bank(name):
            return stack.enter_context(nc.psum_tensor(name, [P, 512], F32))

        def sem(name):
            return stack.enter_context(nc.semaphore(name))

        wout_s = sb("wout_s", [P, KD, D])
        wq_s = sb("wq_s", [P, KD, D])
        wk_s = sb("wk_s", [P, KD, D])
        wvt_s = sb("wvt_s", [P, KD, D])
        wa_s = sb("wa_s", [P, KD, D])
        bqk_s = sb("bqk_s", [P, 4])
        bv_s = sb("bv_s", [S, D])
        bout_s = sb("bout_s", [S, D])
        b1_s = sb("b1_s", [P, FB])
        b2_s = sb("b2_s", [S, D])
        eye_s = sb("eye_s", [P, P])
        eyeb_s = sb("eyeb_s", [P, P], BF16)
        band_s = sb("band_s", [S, S], BF16)
        bandt_s = sb("bandt_s", [S, S], BF16)
        ones_s = sb("ones_s", [P, P])
        mask_i = sb("mask_i", [S, S2], I32)
        mask_s = sb("mask_s", [S, S2])
        x_s = sb("x_s", [S, B, D])
        x1_s = sb("x1_s", [S, B, D])
        xn_s = sb("xn_s", [S, B, D])
        stats = sb("stats", [S, 3, B, 6])
        mv = sb("mv", [S, 3, B, 2])
        var = sb("var", [S, 3, B])
        rstd = sb("rstd", [S, 3, 6, B])
        v_s = sb("v_s", [S, B, NH, DH + 1])
        nmax = sb("nmax", [S, NH])
        shift = sb("shift", [NH, 2, S], BF16)
        pt_s = sb("pt_s", [S, 2, GH, S])
        rec_s = sb("rec_s", [S, NH])
        o_s = sb("o_s", [S, D])
        ot_s = sb("ot_s", [P, KD, S])
        xr_s = sb("xr_s", [S, D])
        xt_s = sb("xt_s", [P, KD, S])
        tt_s = sb("tt_s", [P, KD, S])
        sc_s = sb("sc_s", [S, S2])
        p2_s = sb("p2_s", [S, S2])
        red_s = sb("red_s", [S, 3])
        p2t_s = sb("p2t_s", [CP, CC, S])
        y_s = sb("y_s", [S, D])
        yt_s = sb("yt_s", [P, KD, S])
        w1_s = sb("w1_s", [P, KD, F])
        w2_s = sb("w2_s", [P, FB, D])
        w1_r = sb("w1_r", [P, KD, F], F32R)
        w2_r = sb("w2_r", [P, FB, D], F32R)
        wsum = sb("wsum", [P, 2])
        thr = sb("thr", [P, 2, 3])
        low_s = sb("low_s", [P, 2, TC])

        with ExitStack() as first:
            wqkv_s = sb("wqkv_s", [P, KD, 3 * D], F32, first)
            xn_t = sb("xn_t", [P, KD, T], F32, first)
            part_s = sb("part_s", [P, 2, PARTS, HT], BF16, first)
            rest_s = sb("rest_s", [P, 2, HT], F32, first)
        ctx_r = sb("ctx_r", [CP, B * CC, D])

        with ExitStack() as early:
            q_st = sb("q_st", [QKM, NH, T], BF16, early)
            k_st = sb("k_st", [QKM, NH, T], BF16, early)
            ctx_t = sb("ctx_t", [P, KD, B * S2], F32, early)
        xh_t = sb("xh_t", [P, KD, T], F32R)
        xl_t = sb("xl_t", [P, KD, T], F32R)
        h_s = sb("h_s", [P, 2, HT])
        hh_s = sb("hh_s", [P, FB, HT], F32R)
        hl_s = sb("hl_s", [P, FB, HT], F32R)
        out_s = sb("out_s", [S, B, D])

        parts_d = nc.dram_tensor("parts_d", (2, PARTS, P, 2, T), BF16, kind="Internal").ap()

        banks = [bank(f"bank{i}") for i in range(8)]

        (ld_x, ld_qkv, ld_c, ld_wx, ld_ctx, ld_ff) = map(sem, ("ld_x", "ld_qkv", "ld_c", "ld_wx", "ld_ctx", "ld_ff"))
        ones_ok, vones_ok, kones_ok, mask_ok = map(sem, ("ones_ok", "vones_ok", "kones_ok", "mask_ok"))
        st_ok, mv_ok, var_ok, sq_ok, nr_ok, xn_ok = map(sem, ("st_ok", "mv_ok", "var_ok", "sq_ok", "nr_ok", "xn_ok"))
        xnp_ok, xnt_ok, qkp_ok, p1_ok, r1_ok, p2_ok, r2_ok, p3_ok = map(
            sem, ("xnp_ok", "xnt_ok", "qkp_ok", "p1_ok", "r1_ok", "p2_ok", "r2_ok", "p3_ok"))
        pw_ok = [sem(f"pw_ok{i}") for i in range(2)]
        qk_ld = [sem(f"qk_ld{i}") for i in range(HALVES)]
        vp_ok, v_ok, xb_ok = map(sem, ("vp_ok", "v_ok", "xb_ok"))
        s_ok, max_ok, mt_ok, sh_ok, sl_ok, shift_ld = map(sem, ("s_ok", "max_ok", "mt_ok", "sh_ok", "sl_ok", "shift_ld"))
        stt_ok, exp_ok, pv_ok, rec_ok, o_ok, otp_ok, ot_ok, ao_ok, x1_ok = map(
            sem, ("stt_ok", "exp_ok", "pv_ok", "rec_ok", "o_ok", "otp_ok", "ot_ok", "ao_ok", "x1_ok"))
        wa_p, wa_ok = map(sem, ("wa_p", "wa_ok"))
        xr_ok = sem("xr_ok")
        xtp_ok, xt_ok, ttp_ok, tt_ok, s2_ok, sc_ok, nm2_ok, e2_ok, r2s_ok = map(
            sem, ("xtp_ok", "xt_ok", "ttp_ok", "tt_ok", "s2_ok", "sc_ok", "nm2_ok", "e2_ok", "r2s_ok"))
        ptp_ok, pt_ok, yp_ok, y_ok, ytp_ok, yt_ok, co_ok, x2_ok = map(
            sem, ("ptp_ok", "pt_ok", "yp_ok", "y_ok", "ytp_ok", "yt_ok", "co_ok", "x2_ok"))
        ws_ok, wsp_ok, thr_ok, low_ok, tern_ok = map(sem, ("ws_ok", "wsp_ok", "thr_ok", "low_ok", "tern_ok"))
        x3p_ok, x3h_ok, x3l_ok, hp_ok, h_ok, hh_ok, hl_ok, f_ok, y2_ok, xb2_ok, st_out = map(
            sem, ("x3p_ok", "x3h_ok", "x3l_ok", "hp_ok", "h_ok", "hh_ok", "hl_ok", "f_ok", "y2_ok", "xb2_ok", "st_out"))

        block = stack.enter_context(nc.Block())

        @block.sync
        def _(sp):
            for h in range(HALVES):
                sp.dma_start(x_s[:, HB * h:HB * h + HB, :],
                             x[HB * h:HB * h + HB].rearrange("b s d -> s b d")).then_inc(ld_x, 16)
            sp.dma_start(wqkv_s[:], w_qkv.rearrange("(k p) e -> p k e", p=P)).then_inc(ld_qkv, 16)
            sp.dma_start(bqk_s[:], b_qk).then_inc(ld_qkv, 16)
            sp.dma_start(bv_s[:], b_v.partition_broadcast(S)).then_inc(ld_qkv, 16)
            sp.dma_start(wout_s[:], w_out.rearrange("(k p) e -> p k e", p=P)).then_inc(ld_wx, 16)
            for w, src in ((wq_s, wq), (wk_s, wk), (wvt_s, wv_t)):
                sp.dma_start(w[:], src.rearrange("(k p) e -> p k e", p=P)).then_inc(ld_wx, 16)
            for h in range(HALVES):
                for m in range(4):
                    n = 4 * h + m
                    sp.wait_ge(p3_ok, n + 1)
                    sp.dma_start(parts_d[m // 2, :, :, m % 2, HT * h:HT * h + HT].rearrange("c p t -> p c t"),
                                 part_s[:, n % 2]).then_inc(pw_ok[n % 2], 16)
                    if m % 2:
                        side = m // 2
                        for par in range(2):
                            sp.wait_ge(pw_ok[par], 16 * (2 * h + side + 1))
                        dst, runs = ((q_st, Q_RUNS), (k_st, K_RUNS))[side]
                        for row, part, count in runs:
                            sp.dma_start(
                                dst[DH * row:DH * (row + count), :, HT * h:HT * h + HT],
                                parts_d[side, part:part + count, :, :, HT * h:HT * h + HT].rearrange(
                                    "c (d g) k t -> (c d) (g k) t", d=DH)).then_inc(qk_ld[h], 16)

            def shift_rows(b):
                sp.wait_ge(sl_ok, b + 1)
                for r in range(2):
                    sp.dma_start(q_st[QK + r:QK + r + 1, :, bass.ds(b * S, S)],
                                 shift[:, r, :]).then_inc(shift_ld, 16)

            with sp.Fori(0, B) as b:
                shift_rows(b)
            for h in range(HALVES):
                for b in range(HB * h, HB * h + HB):
                    sp.wait_ge(y2_ok, b + 1)
                    sp.dma_start(out[b], out_s[:, b, :]).then_inc(st_out, 16)
            sp.wait_ge(st_out, 16 * B)

        @block.gpsimd
        def _(pool):
            for dst, src in ((eye_s, eye), (eyeb_s, eye_b), (band_s, band), (bandt_s, band_t), (mask_i, mask),
                             (bout_s, b_out.partition_broadcast(S)), (b2_s, b2.partition_broadcast(S)), (b1_s, b1)):
                pool.dma_start(dst[:], src).then_inc(ld_c, 16)
            pool.memset(ones_s[:], 1.0).then_inc(ones_ok, 1)
            pool.memset(v_s[:, :, :, DH:DH + 1], 1.0).then_inc(vones_ok, 1)
            pool.dma_start(k_st[QK:QKM].rearrange("p h t -> p (h t)"), k_ones).then_inc(kones_ok, 16)
            pool.dma_start(w1_s[:], w1_t.rearrange("(k p) f -> p k f", p=P)).then_inc(ld_ff, 16)
            pool.dma_start(w2_s[:], w2_t.rearrange("(k p) d -> p k d", p=P)).then_inc(ld_ff, 16)
            for k in range(KD):
                pool.dma_start(ctx_t[:, k, :], ctx_cols[P * k:P * k + P, :]).then_inc(ld_ctx, 16)
            for n in range(8):
                pool.wait_ge(r1_ok, n + 1)
                if n >= 2:
                    pool.wait_ge(pw_ok[n % 2], 16 * (n // 2))
                pool.tensor_copy(part_s[:, n % 2, 1, :], rest_s[:, n % 2, :]).then_inc(p2_ok, 1)
                pool.wait_ge(p2_ok, n + 1)
                pool.tensor_tensor(part_s[:, n % 2, 2, :], rest_s[:, n % 2, :], part_s[:, n % 2, 1, :],
                                   ALU.subtract).then_inc(p3_ok, 1)
            pool.wait_ge(qkp_ok, 8)
            pool.wait_ge(vp_ok, B)
            for p in range(2):
                pool.wait_ge(pw_ok[p], 16 * 4)
            for h in range(HALVES):
                pool.dma_start(ctx_r[:, h * 12:h * 12 + 12, :],
                               ctx_rows.rearrange("(c p) d -> p c d", p=CP)[:, h * 12:h * 12 + 12, :]).then_inc(ld_ctx, 16)
            pool.wait_ge(ld_c, 16 * 8)
            pool.wait_ge(xn_ok, B)
            for b in range(B):
                pool.tensor_tensor(x_s[:, b, :], x_s[:, b, :], bout_s[:], ALU.add).then_inc(xb_ok, 1)
            pool.wait_ge(thr_ok, 6)
            for i, (w, r) in enumerate(((w1_s, w1_r), (w2_s, w2_r))):
                wf = w[:].rearrange("p a b -> p (a b)")
                rf = r[:].rearrange("p a b -> p (a b)")
                for c in range(KD * F // TC):
                    n = KD * F // TC * i + c
                    sl = slice(TC * c, TC * c + TC)
                    if n >= 2:
                        pool.wait_ge(tern_ok, n - 1)
                    pool.tensor_scalar(low_s[:, c % 2, :], wf[:, sl], thr[:, i, 2:3], None, ALU.is_lt).then_inc(low_ok, 1)
                    pool.tensor_scalar(wf[:, sl], wf[:, sl], thr[:, i, 1:2], None, ALU.is_gt).then_inc(low_ok, 1)
                    pool.wait_ge(low_ok, 2 * n + 2)
                    pool.tensor_tensor(rf[:, sl], wf[:, sl], low_s[:, c % 2, :], ALU.subtract).then_inc(tern_ok, 1)
            for b in range(B):
                pool.wait_ge(x2_ok, b + 1)
                pool.tensor_tensor(x_s[:, b, :], x1_s[:, b, :], b2_s[:], ALU.add).then_inc(xb2_ok, 1)

        @block.scalar
        def _(act):
            def root(n):
                act.wait_ge(var_ok, n + 1)
                act.activation(rstd[:, n, 0, :], var[:, n, :], ACT.Sqrt).then_inc(sq_ok, 1)

            root(0)
            for h in range(HALVES):
                for k in range(KD):
                    n = KD * h + k
                    act.wait_ge(xnp_ok, n + 1)
                    act.copy(xn_t[:, k, HT * h:HT * h + HT], banks[n % 2][:, 0:HT]).then_inc(xnt_ok, 1)
                if h == 0:
                    act.wait_ge(ld_qkv, 48)
                for m in range(4):
                    n = 4 * h + m
                    act.wait_ge(qkp_ok, n + 1)
                    if n >= 2:
                        act.wait_ge(pw_ok[n % 2], 16 * (n // 2))
                    act.activation(part_s[:, n % 2, 0, :], banks[2 + n % 2][:, 0:HT], ACT.Identity,
                                   bias=bqk_s[:, m:m + 1]).then_inc(p1_ok, 1)
            for k in range(KD):
                act.wait_ge(wa_p, k + 1)
                act.copy(wa_s[:, k, :], banks[6 + k][:, 0:D]).then_inc(wa_ok, 1)

            def a_slot(b, shifts, probs, outs):
                if outs:
                    act.wait_ge(otp_ok, b - 2)
                    if not isinstance(b, int) or b > 3:
                        act.wait_ge(ao_ok, b - 3)
                    act.copy(ot_s[:], banks[6][:, 0:KD * S].rearrange("p (k s) -> p k s", k=KD)).then_inc(ot_ok, 1)
                if probs:
                    for g in range(NG):
                        act.wait_ge(stt_ok, NG * (b - 2) + g + 1)
                        if g >= 2 or not isinstance(b, int) or b > 2:
                            act.wait_ge(pv_ok, NG * (b - 2) + g - 1)
                        act.activation(pt_s[:, g % 2, :, :],
                                       banks[2 + g % 2][0:S, 0:GH * S].rearrange("p (h s) -> p h s", h=GH),
                                       ACT.Exp, scale=DH ** -0.5).then_inc(exp_ok, 1)
                if shifts:
                    act.wait_ge(mt_ok, b + 1)
                    if not isinstance(b, int) or b > 0:
                        act.wait_ge(shift_ld, 32 * b)
                    act.copy(shift[:, 0, :], banks[5][0:NH, 0:S]).then_inc(sh_ok, 1)

            for b in range(4):
                a_slot(b, True, b >= 2, b >= 3)
            with act.Fori(4, B) as b:
                a_slot(b, True, True, True)
            for b in range(B, B + 3):
                a_slot(b, False, b < B + 2, True)

            root(1)

            def x_slot(b, first, second):
                if first:
                    act.wait_ge(xtp_ok, b + 1)
                    if not isinstance(b, int) or b > 0:
                        act.wait_ge(ttp_ok, b)
                    act.copy(xt_s[:], banks[0][:, 0:KD * S].rearrange("p (k s) -> p k s", k=KD)).then_inc(xt_ok, 1)
                if second:
                    act.wait_ge(ptp_ok, b)
                    if not isinstance(b, int) or b > 1:
                        act.wait_ge(yp_ok, b - 1)
                    act.copy(p2t_s[:], banks[3][0:CP, 0:CC * S].rearrange("p (c s) -> p c s", c=CC)).then_inc(pt_ok, 1)
                if first:
                    act.wait_ge(ttp_ok, b + 1)
                    if not isinstance(b, int) or b > 0:
                        act.wait_ge(s2_ok, b)
                    act.copy(tt_s[:], banks[1][:, 0:KD * S].rearrange("p (k s) -> p k s", k=KD)).then_inc(tt_ok, 1)
                if second:
                    act.wait_ge(yp_ok, b)
                    act.wait_ge(r2s_ok, b)
                    if not isinstance(b, int) or b > 1:
                        act.wait_ge(ytp_ok, b - 1)
                    act.activation(y_s[:], banks[4][0:S, 0:D], ACT.Copy, scale=red_s[:, 2:3]).then_inc(y_ok, 1)
                    act.wait_ge(ytp_ok, b)
                    if not isinstance(b, int) or b > 1:
                        act.wait_ge(co_ok, b - 1)
                    act.copy(yt_s[:], banks[5][:, 0:KD * S].rearrange("p (k s) -> p k s", k=KD)).then_inc(yt_ok, 1)
                if first:
                    act.wait_ge(nm2_ok, b + 1)
                    if not isinstance(b, int) or b > 0:
                        act.wait_ge(ptp_ok, b)
                        act.wait_ge(y_ok, b)
                    act.activation(p2_s[:], sc_s[:], ACT.Exp, bias=red_s[:, 0:1],
                                   accum_out=red_s[:, 1:2]).then_inc(e2_ok, 1)

            for b in range(3):
                x_slot(b, True, b >= 1)
            with act.Fori(3, B - 1) as b:
                x_slot(b, True, True)
            x_slot(B - 1, True, True)
            x_slot(B, False, True)

            root(2)
            act.wait_ge(ld_c, 16 * 8)
            for h in range(HALVES):
                for k in range(KD):
                    n = KD * h + k
                    act.wait_ge(x3p_ok, n + 1)
                    act.copy(xh_t[:, k, HT * h:HT * h + HT], banks[n % 2][:, 0:HT]).then_inc(x3h_ok, 1)
                for f in range(FB):
                    n = FB * h + f
                    act.wait_ge(hp_ok, n + 1)
                    if n >= 2:
                        act.wait_ge(hl_ok, n - 1)
                    act.activation(h_s[:, n % 2, :], banks[2 + n % 2][:, 0:HT], ACT.Gelu,
                                   bias=b1_s[:, f:f + 1]).then_inc(h_ok, 1)

        @block.vector
        def _(dve):
            def row_stats(n, b):
                src = x_s if n == 0 else x1_s
                col = bass.ds(b, 1) if not isinstance(b, int) else slice(b, b + 1)
                dve.bn_stats(stats[:, n, col, :].rearrange("p a c -> p (a c)"),
                             src[:, col, :].rearrange("p a c -> p (a c)")).then_inc(st_ok, 1)

            def inverse_root(n):
                r = rstd[:, n]
                for b in range(B):
                    dve.wait_ge(st_ok, B * n + b + 1)
                    dve.bn_aggr(mv[:, n, b, :], stats[:, n, b, :]).then_inc(mv_ok, 1)
                dve.wait_ge(mv_ok, B * n + B)
                dve.tensor_scalar(var[:, n, :], mv[:, n, :, 1], EPS, None, ALU.add).then_inc(var_ok, 1)
                dve.wait_ge(sq_ok, n + 1)
                dve.reciprocal(r[:, 1, :], r[:, 0, :]).then_inc(nr_ok, 1)
                dve.wait_ge(nr_ok, 5 * n + 1)
                dve.tensor_tensor(r[:, 2, :], r[:, 1, :], r[:, 1, :], ALU.mult).then_inc(nr_ok, 1)
                dve.wait_ge(nr_ok, 5 * n + 2)
                dve.tensor_tensor(r[:, 3, :], r[:, 2, :], var[:, n, :], ALU.mult).then_inc(nr_ok, 1)
                dve.wait_ge(nr_ok, 5 * n + 3)
                dve.tensor_scalar(r[:, 4, :], r[:, 3, :], -0.5, 1.5, ALU.mult, ALU.add).then_inc(nr_ok, 1)
                dve.wait_ge(nr_ok, 5 * n + 4)
                dve.tensor_tensor(r[:, 5, :], r[:, 4, :], r[:, 1, :], ALU.mult).then_inc(nr_ok, 1)
                dve.wait_ge(nr_ok, 5 * n + 5)

            def normalize(n, b):
                src = x_s if n == 0 else x1_s
                dve.tensor_scalar(xn_s[:, b, :], src[:, b, :], mv[:, n, b, 0:1], rstd[:, n, 5, b:b + 1],
                                  ALU.subtract, ALU.mult).then_inc(xn_ok, 1)

            for b in range(B):
                if b % HB == 0:
                    dve.wait_ge(ld_x, 32)
                row_stats(0, b)
            inverse_root(0)
            for b in range(B):
                normalize(0, b)
            for h in range(HALVES):
                for m in range(4):
                    n = 4 * h + m
                    dve.wait_ge(p1_ok, n + 1)
                    if n >= 2:
                        dve.wait_ge(p3_ok, n - 1)
                    dve.scalar_tensor_tensor(rest_s[:, n % 2, :], banks[2 + n % 2][:, 0:HT], bqk_s[:, m:m + 1],
                                             part_s[:, n % 2, 0, :], ALU.add, ALU.subtract).then_inc(r1_ok, 1)
                for b in range(HB * h, HB * h + HB):
                    dve.wait_ge(vp_ok, b + 1)
                    dve.tensor_tensor(v_s[:, b, :, 0:DH], banks[4 + b % 2][0:S, 0:D].rearrange("p (h d) -> p h d", h=NH),
                                      bv_s[:].rearrange("p (h d) -> p h d", h=NH), ALU.add).then_inc(v_ok, 1)
            dve.wait_ge(ld_ff, 32)
            for i, w in enumerate((w1_s, w2_s)):
                dve.tensor_reduce(wsum[:, i:i + 1], w[:].rearrange("p a b -> p (a b)"), AX.X, ALU.add,
                                  apply_absolute_value=True).then_inc(ws_ok, 1)
            dve.wait_ge(ld_c, 16 * 8)
            dve.tensor_scalar(mask_s[:], mask_i[:], 0.0, BIG, ALU.is_equal, ALU.mult).then_inc(mask_ok, 1)
            dve.wait_ge(wsp_ok, 1)
            for i in range(2):
                dve.tensor_scalar(thr[:, i, 0:1], banks[5][:, i:i + 1], 1.0 / (F * D), 1e-8,
                                  ALU.mult, ALU.max).then_inc(thr_ok, 1)
                dve.wait_ge(thr_ok, 3 * i + 1)
                for j, c in ((1, 0.5), (2, -0.5)):
                    dve.tensor_scalar(thr[:, i, j:j + 1], thr[:, i, 0:1], c, None, ALU.mult).then_inc(thr_ok, 1)

            def a_slot(b, scores, probs, outs):
                if scores:
                    for g in range(NG):
                        dve.wait_ge(s_ok, NG * b + g + 1)
                        if g == 0 and (not isinstance(b, int) or b > 0):
                            dve.wait_ge(mt_ok, b)
                        dve.tensor_reduce(nmax[:, GH * g:GH * g + GH],
                                          banks[g % 2][0:S, 0:GH * S].rearrange("p (h s) -> p h s", h=GH),
                                          AX.X, ALU.max, negate=True).then_inc(max_ok, 1)
                if outs:
                    dve.wait_ge(ao_ok, b - 2)
                    if isinstance(b, int):
                        dve.wait_ge(xb_ok, b - 2)
                        rows = slice(b - 3, b - 2)
                    else:
                        dve.wait_ge(xb_ok, b - 2)
                        rows = bass.ds(b - 3, 1)
                    dve.tensor_tensor(x1_s[:, rows, :].rearrange("p a c -> p (a c)"), banks[7][0:S, 0:D],
                                      x_s[:, rows, :].rearrange("p a c -> p (a c)"), ALU.add).then_inc(x1_ok, 1)
                    dve.wait_ge(x1_ok, b - 2)
                    row_stats(1, b - 3)
                if scores:
                    dve.wait_ge(sh_ok, b + 1)
                    dve.tensor_tensor(shift[:, 1, :], banks[5][0:NH, 0:S], shift[:, 0, :], ALU.subtract).then_inc(sl_ok, 1)
                if probs:
                    dve.wait_ge(pv_ok, NG * (b - 1))
                    if not isinstance(b, int) or b > 2:
                        dve.wait_ge(otp_ok, b - 2)
                    o = banks[4][0:S, 0:NH * (DH + 1)].rearrange("p (h d) -> p h d", h=NH)
                    dve.reciprocal(rec_s[:], o[:, :, DH]).then_inc(rec_ok, 1)
                    dve.wait_ge(rec_ok, b - 1)
                    dve.tensor_tensor(o_s[:].rearrange("p (h d) -> p h d", h=NH), o[:, :, 0:DH],
                                      rec_s[:].unsqueeze(2).to_broadcast([S, NH, DH]), ALU.mult).then_inc(o_ok, 1)

            for b in range(4):
                a_slot(b, True, b >= 2, b >= 3)
            with dve.Fori(4, B) as b:
                a_slot(b, True, True, True)
            for b in range(B, B + 3):
                a_slot(b, False, b < B + 2, True)

            inverse_root(1)
            def normalize_next(b):
                if not isinstance(b, int) or b > 0:
                    dve.wait_ge(xtp_ok, b)
                one = bass.ds(b, 1)
                dve.tensor_scalar(xr_s[:], x1_s[:, one, :].rearrange("p a c -> p (a c)"),
                                  mv[:, 1, one, 0], rstd[:, 1, 5, one], ALU.subtract, ALU.mult).then_inc(xr_ok, 1)

            normalize_next(0)

            def x_slot(b, first, second, third):
                if first and not (isinstance(b, int) and b == B - 1):
                    normalize_next(b + 1)
                if third:
                    rows = slice(b - 2, b - 1) if isinstance(b, int) else bass.ds(b - 2, 1)
                    row = x1_s[:, rows, :].rearrange("p a c -> p (a c)")
                    dve.wait_ge(co_ok, b - 1)
                    dve.tensor_tensor(row, banks[6][0:S, 0:D], row, ALU.add).then_inc(x2_ok, 1)
                    dve.wait_ge(x2_ok, b - 1)
                    row_stats(2, b - 2)
                if second:
                    dve.wait_ge(e2_ok, b)
                    dve.reciprocal(red_s[:, 2:3], red_s[:, 1:2]).then_inc(r2s_ok, 1)
                if first:
                    if isinstance(b, int) and b == 0:
                        dve.wait_ge(mask_ok, 1)
                    dve.wait_ge(s2_ok, b + 1)
                    if not isinstance(b, int) or b > 0:
                        dve.wait_ge(e2_ok, b)
                    dve.scalar_tensor_tensor(sc_s[:], banks[2][0:S, 0:S2], D ** -0.5, mask_s[:],
                                             ALU.mult, ALU.add).then_inc(sc_ok, 1)
                    dve.wait_ge(sc_ok, b + 1)
                    dve.tensor_reduce(red_s[:, 0:1], sc_s[:], AX.X, ALU.max, negate=True).then_inc(nm2_ok, 1)

            for b in range(3):
                x_slot(b, True, b >= 1, b >= 2)
            with dve.Fori(3, B - 1) as b:
                x_slot(b, True, True, True)
            for b in range(B - 1, B + 2):
                x_slot(b, b < B, b < B + 1, True)

            inverse_root(2)
            dve.wait_ge(xnp_ok, 4)
            for b in range(B):
                normalize(2, b)
            for h in range(HALVES):
                for k in range(KD):
                    n = KD * h + k
                    dve.wait_ge(x3h_ok, n + 1)
                    dve.tensor_tensor(xl_t[:, k, HT * h:HT * h + HT], banks[n % 2][:, 0:HT],
                                      xh_t[:, k, HT * h:HT * h + HT].bitcast(F32), ALU.subtract).then_inc(x3l_ok, 1)
                for f in range(FB):
                    n = FB * h + f
                    dve.wait_ge(h_ok, n + 1)
                    if h and f == 0:
                        dve.wait_ge(f_ok, HB)
                    dve.tensor_copy(hh_s[:, f, :], h_s[:, n % 2, :]).then_inc(hh_ok, 1)
                    dve.wait_ge(hh_ok, n + 1)
                    dve.tensor_tensor(hl_s[:, f, :], h_s[:, n % 2, :], hh_s[:, f, :].bitcast(F32),
                                      ALU.subtract).then_inc(hl_ok, 1)
                for b in range(HB * h, HB * h + HB):
                    dve.wait_ge(f_ok, b + 1)
                    dve.wait_ge(xb2_ok, b + 1)
                    dve.tensor_tensor(out_s[:, b, :], banks[4 + b % 4][0:S, 0:D], x_s[:, b, :], ALU.add).then_inc(y2_ok, 1)

        @block.tensor
        def _(pe):
            pe.wait_ge(ld_c, 16 * 8)
            for h in range(HALVES):
                for k in range(KD):
                    n = KD * h + k
                    if n >= 2:
                        pe.wait_ge(xnt_ok, n - 1)
                    for i in range(HB):
                        pe.wait_ge(xn_ok, HB * h + i + 1)
                        mm = pe.transpose(banks[n % 2][:, S * i:S * i + S],
                                          xn_s[:, HB * h + i, P * k:P * k + P], eye_s[0:S, 0:S])
                    mm.then_inc(xnp_ok, 1)
                if h == 0:
                    pe.wait_ge(ld_qkv, 48)
                pe.wait_ge(xnt_ok, KD * h + KD)
                for m in range(4):
                    n = 4 * h + m
                    if n >= 2:
                        pe.wait_ge(r1_ok, n - 1)
                    for k in range(KD):
                        mm = pe.matmul(banks[2 + n % 2][:, 0:HT], wqkv_s[:, k, P * m:P * m + P],
                                       xn_t[:, k, HT * h:HT * h + HT], start=(k == 0), stop=(k == KD - 1))
                    mm.then_inc(qkp_ok, 1)
                for b in range(HB * h, HB * h + HB):
                    if b >= 2:
                        pe.wait_ge(v_ok, b - 1)
                    for k in range(KD):
                        mm = pe.matmul(banks[4 + b % 2][0:S, 0:D], xn_t[:, k, S * b:S * b + S],
                                       wqkv_s[:, k, 2 * D:3 * D], start=(k == 0), stop=(k == KD - 1))
                    mm.then_inc(vp_ok, 1)
            pe.wait_ge(ld_wx, 64)
            for m in range(KD):
                for k in range(KD):
                    mm = pe.matmul(banks[6 + m][:, 0:D], wq_s[:, k, P * m:P * m + P], wk_s[:, k, :],
                                   start=(k == 0), stop=(k == KD - 1))
                mm.then_inc(wa_p, 1)
            pe.wait_ge(ws_ok, 2)
            pe.wait_ge(ones_ok, 1)
            pe.wait_ge(v_ok, B)
            pe.matmul(banks[5][:, 0:2], ones_s[:], wsum[:], start=True, stop=True).then_inc(wsp_ok, 1)

            def a_slot(b, scores, probs, outs):
                here = bass.ds(b * S, S)
                prev = bass.ds((b - 2) * S, S)
                for g in range(NG):
                    if scores:
                        if g >= 2 or not isinstance(b, int) or b > 0:
                            pe.wait_ge(max_ok, NG * b + g - 1)
                        s = banks[g % 2][0:S, 0:GH * S]
                        pe.matmul(s, eyeb_s[0:S, 0:S], band_s[:].unsqueeze(1).to_broadcast([S, GH, S]),
                                  start=True, stop=False)
                        for i in range(GH):
                            mm = pe.matmul(s[:, S * i:S * i + S], q_st[0:QK, GH * g + i, here],
                                           k_st[0:QK, GH * g + i, here], start=False, stop=(i == GH - 1))
                        mm.then_inc(s_ok, 1)
                    if probs:
                        if g == 0:
                            pe.wait_ge(shift_ld, 32 * (b - 1))
                        if g >= 2 or not isinstance(b, int) or b > 2:
                            pe.wait_ge(exp_ok, NG * (b - 2) + g - 1)
                        s = banks[2 + g % 2][0:S, 0:GH * S]
                        pe.matmul(s, eyeb_s[0:S, 0:S], bandt_s[:].unsqueeze(1).to_broadcast([S, GH, S]),
                                  start=True, stop=False)
                        for i in range(GH):
                            mm = pe.matmul(s[:, S * i:S * i + S], k_st[0:QKM, GH * g + i, prev],
                                           q_st[0:QKM, GH * g + i, prev], start=False, stop=(i == GH - 1))
                        mm.then_inc(stt_ok, 1)
                        if g >= 1:
                            values(b, g - 1)
                    if outs and g == 0:
                        pe.wait_ge(o_ok, b - 2)
                        if not isinstance(b, int) or b > 3:
                            pe.wait_ge(ot_ok, b - 3)
                        for k in range(KD):
                            mm = pe.transpose(banks[6][:, S * k:S * k + S], o_s[:, P * k:P * k + P], eye_s[0:S, 0:S])
                        mm.then_inc(otp_ok, 1)
                    if outs and g == 2:
                        pe.wait_ge(ot_ok, b - 2)
                        if not isinstance(b, int) or b > 3:
                            pe.wait_ge(x1_ok, b - 3)
                        for k in range(KD):
                            mm = pe.matmul(banks[7][0:S, 0:D], ot_s[:, k, :], wout_s[:, k, :],
                                           start=(k == 0), stop=(k == KD - 1))
                        mm.then_inc(ao_ok, 1)
                if scores:
                    pe.wait_ge(max_ok, NG * b + NG)
                    if not isinstance(b, int) or b > 0:
                        pe.wait_ge(sl_ok, b)
                    pe.transpose(banks[5][0:NH, 0:S], nmax[:], eye_s[0:S, 0:S]).then_inc(mt_ok, 1)
                if probs:
                    values(b, NG - 1)

            def values(b, g):
                pe.wait_ge(exp_ok, NG * (b - 2) + g + 1)
                if g == 0 and (not isinstance(b, int) or b > 2):
                    pe.wait_ge(o_ok, b - 2)
                rows = bass.ds(b - 2, 1)
                for i in range(GH):
                    h = GH * g + i
                    mm = pe.matmul(banks[4][0:S, (DH + 1) * h:(DH + 1) * (h + 1)], pt_s[:, g % 2, i, :],
                                   v_s[:, rows, h, :].rearrange("p a c -> p (a c)"), start=True, stop=True)
                mm.then_inc(pv_ok, 1)

            pe.wait_ge(thr_ok, 2 * 3)
            pe.wait_ge(wa_ok, KD)
            pe.wait_ge(r1_ok, 8)
            pe.wait_ge(vones_ok, 1)
            pe.wait_ge(kones_ok, 16)
            for h in range(HALVES):
                pe.wait_ge(qk_ld[h], 16 * (len(Q_RUNS) + len(K_RUNS)))
            for b in range(4):
                a_slot(b, True, b >= 2, b >= 3)
            with pe.Fori(4, B) as b:
                a_slot(b, True, True, True)
            for b in range(B, B + 3):
                a_slot(b, False, b < B + 2, True)

            def x_slot(b, first, second, third):
                if first:
                    pe.wait_ge(xr_ok, b + 1)
                    if not isinstance(b, int) or b > 0:
                        pe.wait_ge(xt_ok, b)
                    for k in range(KD):
                        mm = pe.transpose(banks[0][:, S * k:S * k + S], xr_s[:, P * k:P * k + P], eye_s[0:S, 0:S])
                    mm.then_inc(xtp_ok, 1)
                if third:
                    pe.wait_ge(yt_ok, b - 1)
                    if not isinstance(b, int) or b > 2:
                        pe.wait_ge(x2_ok, b - 2)
                    for k in range(KD):
                        mm = pe.matmul(banks[6][0:S, 0:D], yt_s[:, k, :], wvt_s[:, k, :],
                                       start=(k == 0), stop=(k == KD - 1))
                    mm.then_inc(co_ok, 1)
                if second:
                    pe.wait_ge(e2_ok, b)
                    if not isinstance(b, int) or b > 1:
                        pe.wait_ge(pt_ok, b - 1)
                    for c in range(CC):
                        mm = pe.transpose(banks[3][0:CP, S * c:S * c + S], p2_s[:, CP * c:CP * c + CP], eye_s[0:S, 0:S])
                    mm.then_inc(ptp_ok, 1)
                if first:
                    pe.wait_ge(xt_ok, b + 1)
                    if not isinstance(b, int) or b > 0:
                        pe.wait_ge(tt_ok, b)
                    for m in range(KD):
                        for k in range(KD):
                            mm = pe.matmul(banks[1][:, S * m:S * m + S], wa_s[:, k, P * m:P * m + P], xt_s[:, k, :],
                                           start=(k == 0), stop=(k == KD - 1))
                    mm.then_inc(ttp_ok, 1)
                if second:
                    pe.wait_ge(pt_ok, b)
                    if not isinstance(b, int) or b > 1:
                        pe.wait_ge(y_ok, b - 1)
                    for c in range(CC):
                        mm = pe.matmul(banks[4][0:S, 0:D], p2t_s[:, c, :],
                                       ctx_r[:, bass.ds((b - 1) * CC + c, 1), :].rearrange("p a c -> p (a c)"),
                                       start=(c == 0), stop=(c == CC - 1))
                    mm.then_inc(yp_ok, 1)
                if first:
                    pe.wait_ge(tt_ok, b + 1)
                    if not isinstance(b, int) or b > 0:
                        pe.wait_ge(sc_ok, b)
                    for k in range(KD):
                        mm = pe.matmul(banks[2][0:S, 0:S2], tt_s[:, k, :], ctx_t[:, k, bass.ds(b * S2, S2)],
                                       start=(k == 0), stop=(k == KD - 1))
                    mm.then_inc(s2_ok, 1)
                if second:
                    pe.wait_ge(y_ok, b)
                    if not isinstance(b, int) or b > 1:
                        pe.wait_ge(yt_ok, b - 1)
                    for k in range(KD):
                        mm = pe.transpose(banks[5][:, S * k:S * k + S], y_s[:, P * k:P * k + P], eye_s[0:S, 0:S])
                    mm.then_inc(ytp_ok, 1)

            pe.wait_ge(ld_ctx, 64)
            for b in range(3):
                x_slot(b, True, b >= 1, b >= 2)
            with pe.Fori(3, B - 1) as b:
                x_slot(b, True, True, True)
            for b in range(B - 1, B + 2):
                x_slot(b, b < B, b < B + 1, True)

            def ffn_in(h):
                for k in range(KD):
                    n = KD * h + k
                    if n >= 2:
                        pe.wait_ge(x3l_ok, n - 1)
                    for i in range(HB):
                        pe.wait_ge(xn_ok, B + HB * h + i + 1)
                        mm = pe.transpose(banks[n % 2][:, S * i:S * i + S],
                                          xn_s[:, HB * h + i, P * k:P * k + P], eye_s[0:S, 0:S])
                    mm.then_inc(x3p_ok, 1)

            def ffn_hidden(h):
                pe.wait_ge(x3l_ok, KD * h + KD)
                for f in range(FB):
                    n = FB * h + f
                    if n >= 2:
                        pe.wait_ge(h_ok, n - 1)
                    for k in range(KD):
                        for j, xp in enumerate((xh_t, xl_t)):
                            mm = pe.matmul(banks[2 + n % 2][:, 0:HT], w1_r[:, k, P * f:P * f + P],
                                           xp[:, k, HT * h:HT * h + HT], start=(k == 0 and j == 0),
                                           stop=(k == KD - 1 and j == 1))
                    mm.then_inc(hp_ok, 1)

            def ffn_out(h):
                for b in range(HB * h, HB * h + HB):
                    i = b - HB * h
                    if h:
                        pe.wait_ge(y2_ok, b - 3)
                    for f in range(FB):
                        pe.wait_ge(hl_ok, FB * h + f + 1)
                        for j, hp in enumerate((hh_s, hl_s)):
                            mm = pe.matmul(banks[4 + b % 4][0:S, 0:D], hp[:, f, S * i:S * i + S], w2_r[:, f, :],
                                           start=(f == 0 and j == 0), stop=(f == FB - 1 and j == 1))
                    mm.then_inc(f_ok, 1)

            pe.wait_ge(tern_ok, 2 * KD * F // TC)
            ffn_in(0)
            ffn_in(1)
            ffn_hidden(0)
            ffn_out(0)
            ffn_hidden(1)
            ffn_out(1)


def kernel(**inputs):
    import numpy as np
    import concourse.bacc as bacc
    from concourse.bass_utils import run_bass_kernel_spmd as run

    def rows(a):
        return np.ascontiguousarray(a)

    order = np.array([side * D + (2 * g + k) * DH + d
                      for side in range(2) for k in range(2) for d in range(DH) for g in range(NH // 2)])
    w_qkv = np.asarray(inputs["L0_attn_w_qkv"])
    b_qkv = np.asarray(inputs["L0_attn_b_qkv"])
    i, j = np.arange(S)[:, None], np.arange(S)[None, :]
    allowed = (j % STRIDE == 0) | (np.abs(i - j) <= WINDOW)
    bf16 = mybir.dt.np(BF16)
    band = np.where(allowed, 0.0, BIG).astype(bf16)
    ctx = np.asarray(inputs["ctx_1024"]).reshape(B * S2, D)
    arrays = {
        "x": rows(inputs["x"]),
        "ctx_rows": rows(ctx),
        "ctx_cols": rows(ctx.T),
        "mask": rows(inputs["mask_SxS2_ik0"]),
        "w_qkv": rows(np.concatenate([w_qkv[:, order], w_qkv[:, 2 * D:]], axis=1)),
        "b_qk": rows(b_qkv[order].reshape(4, P).T),
        "b_v": rows(b_qkv[2 * D:]),
        "w_out": rows(inputs["L0_attn_w_out"]),
        "b_out": rows(inputs["L0_attn_b_out"]),
        "wq": rows(inputs["L0_xattn_Wq"]),
        "wk": rows(inputs["L0_xattn_Wk"]),
        "wv_t": rows(np.asarray(inputs["L0_xattn_Wv"]).T),
        "w1_t": rows(np.asarray(inputs["L0_ffn_W1"]).T),
        "b1": rows(np.asarray(inputs["L0_ffn_b1"]).reshape(FB, P).T),
        "w2_t": rows(np.asarray(inputs["L0_ffn_W2"]).T),
        "b2": rows(inputs["L0_ffn_b2"]),
        "eye": np.eye(P, dtype=np.float32),
        "eye_b": np.eye(P).astype(bf16),
        "k_ones": np.ones((QKM - QK, NH * T), dtype=bf16),
        "band": band,
        "band_t": rows(band.T),
    }
    nc = bacc.Bacc("TRN2", target_bir_lowering=False, num_devices=1)
    aps = {name: nc.dram_tensor(name, a.shape, mybir.dt.from_np(a.dtype), kind="ExternalInput").ap()
           for name, a in arrays.items()}
    out = nc.dram_tensor("out", (B, S, D), F32, kind="ExternalOutput").ap()
    build(nc, out=out, **aps)
    return run(nc, [arrays], core_ids=[0]).results[0]["out"]
```

```python
from contextlib import ExitStack

import concourse.bass as bass
from concourse import mybir

ALU = mybir.AluOpType
ACT = mybir.ActivationFunctionType
AX = mybir.AxisListType
F32 = mybir.dt.float32
F32R = mybir.dt.float32r
BF16 = mybir.dt.bfloat16
I32 = mybir.dt.int32

B, S, D = 8, 112, 256
T = B * S
P = 128
KD = D // P
NH, DH = 16, 16
S2 = 375
CC, CP = 3, 125
F = 1024
FB = F // P
TC = 512
HALVES = 2
HB = B // HALVES
HT = HB * S
NG, GH = 4, 4
QUAD = 32
MAGIC = 0x5F3759DF
STRIDE, WINDOW = 32, 64
EPS = 1e-5
BIG = -1.0e30
PARTS = 3
QK = 6 * DH
QKM = QK + 2
Q_RUNS = [(0, 0, 3), (3, 0, 2), (5, 0, 1)]
K_RUNS = [(b, p, 1) for b, p in enumerate((0, 0, 0, 1, 1, 2))]


def build(nc, x, ctx_rows, ctx_cols, mask, w_qkv, b_qk, b_v, w_out, b_out, wq, wk, wv_t,
          w1_t, b1, w2_t, b2, eye, eye_b, k_ones, band, band_t, out):
    with ExitStack() as stack:
        def sb(name, shape, dt=F32, where=stack):
            return where.enter_context(nc.sbuf_tensor(name, shape, dt))

        def bank(name):
            return stack.enter_context(nc.psum_tensor(name, [P, 512], F32))

        def sem(name):
            return stack.enter_context(nc.semaphore(name))

        wout_s = sb("wout_s", [P, KD, D])
        wq_s = sb("wq_s", [P, KD, D])
        wk_s = sb("wk_s", [P, KD, D])
        wvt_s = sb("wvt_s", [P, KD, D])
        wa_s = sb("wa_s", [P, KD, D])
        bqk_s = sb("bqk_s", [P, 4])
        bv_s = sb("bv_s", [S, D])
        bout_s = sb("bout_s", [S, D])
        b1_s = sb("b1_s", [P, FB])
        b2_s = sb("b2_s", [S, D])
        eye_s = sb("eye_s", [P, P])
        eyeb_s = sb("eyeb_s", [P, P], BF16)
        band_s = sb("band_s", [S, S], BF16)
        bandt_s = sb("bandt_s", [S, S], BF16)
        ones_s = sb("ones_s", [P, P])
        mask_i = sb("mask_i", [S, S2], I32)
        mask_s = sb("mask_s", [S, S2])
        x_s = sb("x_s", [S, B, D])
        x1_s = sb("x1_s", [S, B, D])
        xn_s = sb("xn_s", [S, B, D])
        stats = sb("stats", [S, 3, B, 6])
        mv = sb("mv", [S, 3, B, 2])
        var = sb("var", [S, 3, B])
        root = sb("root", [S, 3, 4, B])
        tmp = sb("tmp", [S, 2, B])
        v_s = sb("v_s", [S, B, NH, DH + 1])
        nmax = sb("nmax", [S, NH])
        shift = sb("shift", [NH, 2, S], BF16)
        pt_s = sb("pt_s", [S, 2, GH, S])
        ov_s = sb("ov_s", [P, NG, S])
        rec_s = sb("rec_s", [S, NH])
        o_s = sb("o_s", [S, D])
        ot_s = sb("ot_s", [P, KD, S])
        xr_s = sb("xr_s", [S, D])
        xt_s = sb("xt_s", [P, KD, S])
        tt_s = sb("tt_s", [P, KD, S])
        sc_s = sb("sc_s", [S, S2])
        p2_s = sb("p2_s", [S, S2])
        red_s = sb("red_s", [S, 2])
        rec2_s = sb("rec2_s", [S, 2])
        p2t_s = sb("p2t_s", [CP, CC, S])
        y_s = sb("y_s", [S, D])
        yt_s = sb("yt_s", [P, KD, S])
        w1_s = sb("w1_s", [P, KD, F])
        w2_s = sb("w2_s", [P, FB, D])
        w1_r = sb("w1_r", [P, KD, F], F32R)
        w2_r = sb("w2_r", [P, FB, D], F32R)
        wsum = sb("wsum", [P, 2, 2])
        thr = sb("thr", [P, 2, 3])
        low_s = sb("low_s", [P, 2, TC])

        with ExitStack() as first:
            wqkv_s = sb("wqkv_s", [P, KD, 3 * D], F32, first)
            xn_t = sb("xn_t", [P, KD, T], F32, first)
            part_s = sb("part_s", [P, 2, PARTS, HT], BF16, first)
            rest_s = sb("rest_s", [P, 2, HT], F32, first)
        ctx_r = sb("ctx_r", [CP, B * CC, D])

        with ExitStack() as early:
            q_st = sb("q_st", [QKM, NH, T], BF16, early)
            k_st = sb("k_st", [QKM, NH, T], BF16, early)
            ctx_t = sb("ctx_t", [P, KD, B * S2], F32, early)
        xh_t = sb("xh_t", [P, KD, T], F32R)
        xl_t = sb("xl_t", [P, KD, T], F32R)
        h_s = sb("h_s", [P, 2, HT])
        hh_s = sb("hh_s", [P, FB, T], F32R)
        hl_s = sb("hl_s", [P, FB, T], F32R)

        parts_d = nc.dram_tensor("parts_d", (2, PARTS, P, 2, T), BF16, kind="Internal").ap()

        banks = [bank(f"bank{i}") for i in range(8)]

        def sems(names):
            return [sem(n) for n in names.split()]

        ld_eye, ld_x0, ld_x1, ld_qk, ld_v, ld_c, ld_wx, ld_ctx = sems(
            "ld_eye ld_x0 ld_x1 ld_qk ld_v ld_c ld_wx ld_ctx")
        ld_x = [ld_x0, ld_x1]
        ld_w = sems("ld_w1 ld_w2")
        ones_ok, vones_ok, kones_ok, mask_ok, ovz_ok = sems("ones_ok vones_ok kones_ok mask_ok ovz_ok")
        st_ok, mv_ok, var_ok, root_ok, xn_ok = sems("st_ok mv_ok var_ok root_ok xn_ok")
        xnp_ok, xnt_ok, qkp_ok, p1_ok, r1_ok, p2_ok, p3_ok, vp_ok, v_ok, xb_ok = sems(
            "xnp_ok xnt_ok qkp_ok p1_ok r1_ok p2_ok p3_ok vp_ok v_ok xb_ok")
        pw_ok = sems("pw_ok0 pw_ok1")
        qk_ld = sems("qk_ld0 qk_ld1")
        wa_p, wa_ok, ws_ok, wsp_ok, thr_sum, thr_ok, low_ok, tern_ok = sems(
            "wa_p wa_ok ws_ok wsp_ok thr_sum thr_ok low_ok tern_ok")
        s_ok, max_ok, mt_ok, sh_ok, sl_ok, shift_ld = sems("s_ok max_ok mt_ok sh_ok sl_ok shift_ld")
        st_p, exp_ok, pv_ok, ov_ok, op_ok, rec_ok, o_ok, otp_ok, ot_ok, ao_ok, x1_ok = sems(
            "st_p exp_ok pv_ok ov_ok op_ok rec_ok o_ok otp_ok ot_ok ao_ok x1_ok")
        xr_ok, xtp_ok, xt_ok, ttp_ok, tt_ok, s2_ok, sc_ok, nm2_ok, e2_ok, r2_ok = sems(
            "xr_ok xtp_ok xt_ok ttp_ok tt_ok s2_ok sc_ok nm2_ok e2_ok r2_ok")
        ptp_ok, pt_ok, yp_ok, y_ok, ytp_ok, yt_ok, co_ok, x2_ok = sems(
            "ptp_ok pt_ok yp_ok y_ok ytp_ok yt_ok co_ok x2_ok")
        x3p_ok, x3h_ok, x3l_ok, hp_ok, h_ok, hh_ok, hl_ok, f_ok, y2_ok, xb2_ok, st_out = sems(
            "x3p_ok x3h_ok x3l_ok hp_ok h_ok hh_ok hl_ok f_ok y2_ok xb2_ok st_out")

        def after(eng, signal, count):
            if count > 0:
                eng.wait_ge(signal, count)

        V0, OV, OP, SMALL, AO = 4, 4, 5, 6, 7
        XT, TT, SC, PT, YY, YT, CO = 0, 1, 2, 3, 4, 5, 6
        HID = (2, 7)
        OUT = (3, 4, 5, 6)

        block = stack.enter_context(nc.Block())

        @block.sync
        def _(sp):
            for h in range(HALVES):
                sp.dma_start(x_s[:, HB * h:HB * h + HB, :],
                             x[HB * h:HB * h + HB].rearrange("b s d -> s b d")).then_inc(ld_x[h], 16)
                if h == 0:
                    sp.dma_start(wqkv_s[:, :, 0:2 * D],
                                 w_qkv[:, 0:2 * D].rearrange("(k p) e -> p k e", p=P)).then_inc(ld_qk, 16)
                    sp.dma_start(bqk_s[:], b_qk).then_inc(ld_qk, 16)
            sp.dma_start(wqkv_s[:, :, 2 * D:3 * D],
                         w_qkv[:, 2 * D:3 * D].rearrange("(k p) e -> p k e", p=P)).then_inc(ld_v, 16)
            sp.dma_start(bv_s[:], b_v.partition_broadcast(S)).then_inc(ld_v, 16)
            for w, src in ((wq_s, wq), (wk_s, wk), (wvt_s, wv_t), (wout_s, w_out)):
                sp.dma_start(w[:], src.rearrange("(k p) e -> p k e", p=P)).then_inc(ld_wx, 16)
            for h in range(HALVES):
                for m in range(4):
                    n = 4 * h + m
                    sp.wait_ge(p3_ok, n + 1)
                    sp.dma_start(parts_d[m // 2, :, :, m % 2, HT * h:HT * h + HT].rearrange("c p t -> p c t"),
                                 part_s[:, n % 2]).then_inc(pw_ok[n % 2], 16)
                    if m % 2:
                        side = m // 2
                        for p in range(2):
                            sp.wait_ge(pw_ok[p], 16 * (2 * h + side + 1))
                        dst, runs = ((q_st, Q_RUNS), (k_st, K_RUNS))[side]
                        for row, part, count in runs:
                            sp.dma_start(
                                dst[DH * row:DH * (row + count), :, HT * h:HT * h + HT],
                                parts_d[side, part:part + count, :, :, HT * h:HT * h + HT].rearrange(
                                    "c (d g) k t -> (c d) (g k) t", d=DH)).then_inc(qk_ld[h], 16)
            for b in range(B):
                sp.wait_ge(sl_ok, b + 1)
                for r in range(2):
                    sp.dma_start(q_st[QK + r:QK + r + 1, :, S * b:S * b + S],
                                 shift[:, r, :]).then_inc(shift_ld, 16)
            for b in range(B):
                sp.wait_ge(y2_ok, b + 1)
                sp.dma_start(out[b], x_s[:, b, :]).then_inc(st_out, 16)
            sp.wait_ge(st_out, 16 * B)

        @block.gpsimd
        def _(pool):
            pool.dma_start(eye_s[:], eye).then_inc(ld_eye, 16)
            for dst, src in ((eyeb_s, eye_b), (band_s, band), (bandt_s, band_t), (mask_i, mask),
                             (bout_s, b_out.partition_broadcast(S)), (b2_s, b2.partition_broadcast(S)), (b1_s, b1)):
                pool.dma_start(dst[:], src).then_inc(ld_c, 16)
            pool.memset(ones_s[:], 1.0).then_inc(ones_ok, 1)
            pool.memset(v_s[:, :, :, DH:DH + 1], 1.0).then_inc(vones_ok, 1)
            pool.dma_start(k_st[QK:QKM].rearrange("p h t -> p (h t)"), k_ones).then_inc(kones_ok, 16)
            pool.wait_ge(qk_ld[0], 16 * (len(Q_RUNS) + len(K_RUNS)))
            pool.dma_start(w1_s[:], w1_t.rearrange("(k p) f -> p k f", p=P)).then_inc(ld_w[0], 16)
            pool.wait_ge(qk_ld[1], 16 * (len(Q_RUNS) + len(K_RUNS)))
            pool.dma_start(w2_s[:], w2_t.rearrange("(k p) d -> p k d", p=P)).then_inc(ld_w[1], 16)
            for k in range(KD):
                pool.dma_start(ctx_t[:, k, :], ctx_cols[P * k:P * k + P, :]).then_inc(ld_ctx, 16)
            pool.wait_ge(qkp_ok, 8)
            pool.wait_ge(vp_ok, B)
            for p in range(2):
                pool.wait_ge(pw_ok[p], 16 * 4)
            pool.wait_ge(p3_ok, 8)
            for h in range(HALVES):
                n = B * CC // HALVES
                pool.dma_start(ctx_r[:, n * h:n * h + n, :],
                               ctx_rows.rearrange("(c p) d -> p c d", p=CP)[:, n * h:n * h + n, :]).then_inc(ld_ctx, 16)
            pool.wait_ge(ld_c, 16 * 7)
            pool.wait_ge(xn_ok, B)
            for b in range(B):
                pool.tensor_tensor(x_s[:, b, :], x_s[:, b, :], bout_s[:], ALU.add).then_inc(xb_ok, 1)
            pool.wait_ge(thr_ok, 4)
            for i, (w, t) in enumerate(((w1_s, w1_r), (w2_s, w2_r))):
                wf = w[:].rearrange("p a b -> p (a b)")
                tf = t[:].rearrange("p a b -> p (a b)")
                for c in range(KD * F // TC):
                    n = KD * F // TC * i + c
                    sl = slice(TC * c, TC * c + TC)
                    after(pool, tern_ok, n - 1)
                    pool.tensor_scalar(low_s[:, c % 2, :], wf[:, sl], thr[:, i, 2:3], None, ALU.is_lt).then_inc(low_ok, 1)
                    pool.tensor_scalar(wf[:, sl], wf[:, sl], thr[:, i, 1:2], None, ALU.is_gt).then_inc(low_ok, 1)
                    pool.wait_ge(low_ok, 2 * n + 2)
                    pool.tensor_tensor(tf[:, sl], wf[:, sl], low_s[:, c % 2, :], ALU.subtract).then_inc(tern_ok, 1)
            for b in range(B):
                pool.wait_ge(x2_ok, b + 1)
                pool.tensor_tensor(x_s[:, b, :], x1_s[:, b, :], b2_s[:], ALU.add).then_inc(xb2_ok, 1)

        @block.scalar
        def _(act):
            def wide(n):
                return banks[n][:, 0:KD * S].rearrange("p (k s) -> p k s", k=KD)

            act.wait_ge(ld_qk, 32)
            for h in range(HALVES):
                for k in range(KD):
                    act.wait_ge(xnp_ok, KD * h + k + 1)
                    act.copy(xn_t[:, k, HT * h:HT * h + HT], banks[k][:, 0:HT]).then_inc(xnt_ok, 1)
                for m in range(4):
                    n = 4 * h + m
                    act.wait_ge(qkp_ok, n + 1)
                    after(act, pw_ok[n % 2], 16 * (n // 2))
                    act.activation(part_s[:, n % 2, 0, :], banks[2 + n % 2][:, 0:HT], ACT.Identity,
                                   bias=bqk_s[:, m:m + 1]).then_inc(p1_ok, 1)
                    act.wait_ge(r1_ok, n + 1)
                    act.copy(part_s[:, n % 2, 1, :], rest_s[:, n % 2, :]).then_inc(p2_ok, 1)
            for k in range(KD):
                act.wait_ge(wa_p, k + 1)
                act.copy(wa_s[:, k, :], banks[6 + k][:, 0:D]).then_inc(wa_ok, 1)

            def shift_high(b):
                act.wait_ge(mt_ok, b + 1)
                after(act, shift_ld, 32 * b)
                act.copy(shift[:, 0, :], banks[SMALL][0:NH, 0:S]).then_inc(sh_ok, 1)

            def values_out(b):
                act.wait_ge(pv_ok, NG * b + NG)
                after(act, op_ok, b)
                act.copy(ov_s[:], banks[OV][:, 0:NG * S].rearrange("p (g s) -> p g s", g=NG)).then_inc(ov_ok, 1)

            def probs(b, g):
                n = NG * b + g
                act.wait_ge(st_p, n + 1)
                after(act, pv_ok, n - 1)
                act.activation(pt_s[:, g % 2, :, :],
                               banks[2 + g % 2][0:S, 0:GH * S].rearrange("p (h s) -> p h s", h=GH),
                               ACT.Exp, scale=DH ** -0.5).then_inc(exp_ok, 1)

            def heads_out(b):
                act.wait_ge(otp_ok, b + 1)
                after(act, ao_ok, b)
                act.copy(ot_s[:], wide(SMALL)).then_inc(ot_ok, 1)

            def a_slot(b):
                if 0 <= b - 1 < B:
                    shift_high(b - 1)
                if 0 <= b - 3 < B:
                    values_out(b - 3)
                if 0 <= b - 2 < B:
                    probs(b - 2, 0)
                    probs(b - 2, 1)
                if 0 <= b - 3 < B:
                    heads_out(b - 3)
                if 0 <= b - 2 < B:
                    probs(b - 2, 2)
                    probs(b - 2, 3)

            def norm_out(b):
                act.wait_ge(xtp_ok, b + 1)
                after(act, ttp_ok, b)
                act.copy(xt_s[:], wide(XT)).then_inc(xt_ok, 1)

            def query_out(b):
                act.wait_ge(ttp_ok, b + 1)
                after(act, s2_ok, b)
                act.copy(tt_s[:], wide(TT)).then_inc(tt_ok, 1)

            def x_slot(b):
                if 0 <= b - 1 < B:
                    act.wait_ge(ptp_ok, b)
                    after(act, yp_ok, b - 1)
                    act.copy(p2t_s[:], banks[PT][0:CP, 0:CC * S].rearrange("p (c s) -> p c s", c=CC)).then_inc(pt_ok, 1)
                if b + 1 < B:
                    norm_out(b + 1)
                if b < B:
                    act.wait_ge(nm2_ok, b + 1)
                    after(act, ptp_ok, b)
                    after(act, r2_ok, b)
                    act.activation(p2_s[:], sc_s[:], ACT.Exp, bias=red_s[:, 0:1],
                                   accum_out=red_s[:, 1:2]).then_inc(e2_ok, 1)
                if 0 <= b - 1 < B:
                    act.wait_ge(yp_ok, b)
                    act.wait_ge(r2_ok, b)
                    after(act, ytp_ok, b - 1)
                    act.activation(y_s[:], banks[YY][0:S, 0:D], ACT.Copy,
                                   scale=rec2_s[:, (b - 1) % 2:(b - 1) % 2 + 1]).then_inc(y_ok, 1)
                if b + 1 < B:
                    query_out(b + 1)
                if 0 <= b - 1 < B:
                    act.wait_ge(ytp_ok, b)
                    after(act, co_ok, b - 1)
                    act.copy(yt_s[:], wide(YT)).then_inc(yt_ok, 1)

            def ffn_in(h):
                for k in range(KD):
                    act.wait_ge(x3p_ok, KD * h + k + 1)
                    act.copy(xh_t[:, k, HT * h:HT * h + HT], banks[k][:, 0:HT]).then_inc(x3h_ok, 1)

            def ffn_hidden(h, f):
                n = FB * h + f
                act.wait_ge(hp_ok, n + 1)
                after(act, hl_ok, n - 1)
                act.activation(h_s[:, n % 2, :], banks[HID[n % 2]][:, 0:HT], ACT.Gelu,
                               bias=b1_s[:, f:f + 1]).then_inc(h_ok, 1)

            for b in range(B + 1):
                a_slot(b)
            norm_out(0)
            a_slot(B + 1)
            query_out(0)
            a_slot(B + 2)
            for b in range(B + 1):
                if b == B:
                    ffn_in(0)
                x_slot(b)
            act.wait_ge(ld_c, 16 * 7)
            for f in range(FB):
                ffn_hidden(0, f)
            ffn_in(1)
            for f in range(FB):
                ffn_hidden(1, f)

        @block.vector
        def _(dve):
            def row_stats(n, b):
                dve.bn_stats(stats[:, n, b, :], (x_s if n == 0 else x1_s)[:, b, :]).then_inc(st_ok, 1)

            def inverse_root(n, h):
                cols = slice(HB * h, HB * h + HB)
                call = HALVES * n + h
                dve.wait_ge(st_ok, HB * (call + 1))
                for b in range(HB * h, HB * h + HB):
                    dve.bn_aggr(mv[:, n, b, :], stats[:, n, b, :]).then_inc(mv_ok, 1)
                dve.wait_ge(mv_ok, HB * (call + 1))
                v = var[:, n, cols]
                dve.tensor_scalar(v, mv[:, n, cols, 1], EPS, None, ALU.add).then_inc(var_ok, 1)
                dve.wait_ge(var_ok, call + 1)
                dve.tensor_scalar(root[:, n, 0, cols].bitcast(I32), v.bitcast(I32), -0.5, float(MAGIC),
                                  ALU.mult, ALU.add).then_inc(root_ok, 1)
                for i in range(3):
                    y, done = root[:, n, i, cols], 10 * call + 3 * i
                    dve.wait_ge(root_ok, done + 1)
                    dve.tensor_tensor(tmp[:, 0, cols], y, y, ALU.mult).then_inc(root_ok, 1)
                    dve.wait_ge(root_ok, done + 2)
                    dve.scalar_tensor_tensor(tmp[:, 1, cols], tmp[:, 0, cols], -0.5, v,
                                             ALU.mult, ALU.mult).then_inc(root_ok, 1)
                    dve.wait_ge(root_ok, done + 3)
                    dve.scalar_tensor_tensor(root[:, n, i + 1, cols], tmp[:, 1, cols], 1.5, y,
                                             ALU.add, ALU.mult).then_inc(root_ok, 1)
                dve.wait_ge(root_ok, 10 * (call + 1))

            def normalize(dst, n, b, signal):
                dve.tensor_scalar(dst, (x_s if n == 0 else x1_s)[:, b, :], mv[:, n, b, 0:1], root[:, n, 3, b:b + 1],
                                  ALU.subtract, ALU.mult).then_inc(signal, 1)

            for h in range(HALVES):
                dve.wait_ge(ld_x[h], 16)
                for b in range(HB * h, HB * h + HB):
                    row_stats(0, b)
                inverse_root(0, h)
                for b in range(HB * h, HB * h + HB):
                    normalize(xn_s[:, b, :], 0, b, xn_ok)
            for n in range(8):
                dve.wait_ge(p1_ok, n + 1)
                dve.scalar_tensor_tensor(rest_s[:, n % 2, :], banks[2 + n % 2][:, 0:HT], bqk_s[:, n % 4:n % 4 + 1],
                                         part_s[:, n % 2, 0, :], ALU.add, ALU.subtract).then_inc(r1_ok, 1)
                dve.wait_ge(p2_ok, n + 1)
                dve.tensor_tensor(part_s[:, n % 2, 2, :], rest_s[:, n % 2, :], part_s[:, n % 2, 1, :],
                                  ALU.subtract).then_inc(p3_ok, 1)
            dve.wait_ge(ld_v, 32)
            for b in range(B):
                dve.wait_ge(vp_ok, b + 1)
                dve.tensor_tensor(v_s[:, b, :, 0:DH], banks[V0 + b % 2][0:S, 0:D].rearrange("p (h d) -> p h d", h=NH),
                                  bv_s[:].rearrange("p (h d) -> p h d", h=NH), ALU.add).then_inc(v_ok, 1)
            dve.wait_ge(v_ok, B)
            dve.memset(banks[OV][:, 0:NG * S], 0.0).then_inc(ovz_ok, 1)
            dve.wait_ge(ld_c, 16 * 7)
            dve.tensor_scalar(mask_s[:], mask_i[:], 0.0, BIG, ALU.is_equal, ALU.mult).then_inc(mask_ok, 1)

            def weight_sum(i, k):
                dve.wait_ge(ld_w[i], 16)
                w = (w1_s, w2_s)[i]
                dve.tensor_reduce(wsum[:, i, k:k + 1], w[:].rearrange("p a b -> p (a b)")[:, F * k:F * k + F],
                                  AX.X, ALU.add, apply_absolute_value=True).then_inc(ws_ok, 1)

            def thresholds():
                dve.wait_ge(wsp_ok, 1)
                for i in range(2):
                    dve.tensor_reduce(thr[:, i, 0:1], banks[AO][:, 2 * i:2 * i + 2], AX.X, ALU.add).then_inc(thr_sum, 1)
                    dve.wait_ge(thr_sum, 2 * i + 1)
                    dve.tensor_scalar(thr[:, i, 0:1], thr[:, i, 0:1], 1.0 / (F * D), 1e-8,
                                      ALU.mult, ALU.max).then_inc(thr_sum, 1)
                    dve.wait_ge(thr_sum, 2 * i + 2)
                    for j, c in ((1, 0.5), (2, -0.5)):
                        dve.tensor_scalar(thr[:, i, j:j + 1], thr[:, i, 0:1], c, None, ALU.mult).then_inc(thr_ok, 1)

            def shift_low(b):
                dve.wait_ge(sh_ok, b + 1)
                dve.tensor_tensor(shift[:, 1, :], banks[SMALL][0:NH, 0:S], shift[:, 0, :], ALU.subtract).then_inc(sl_ok, 1)

            def row_max(b, g):
                dve.wait_ge(s_ok, NG * b + g + 1)
                if g == 0:
                    after(dve, mt_ok, b)
                dve.tensor_reduce(nmax[:, GH * g:GH * g + GH],
                                  banks[g % 2][0:S, 0:GH * S].rearrange("p (h s) -> p h s", h=GH),
                                  AX.X, ALU.max, negate=True).then_inc(max_ok, 1)

            def divide(b):
                dve.wait_ge(op_ok, b + 1)
                after(dve, otp_ok, b)
                o = banks[OP][0:S, :].rearrange("p (h d) -> p h d", d=QUAD)
                dve.reciprocal(rec_s[:], o[:, :, DH]).then_inc(rec_ok, 1)
                dve.wait_ge(rec_ok, b + 1)
                dve.tensor_tensor(o_s[:].rearrange("p (h d) -> p h d", h=NH), o[:, :, 0:DH],
                                  rec_s[:].unsqueeze(2).to_broadcast([S, NH, DH]), ALU.mult).then_inc(o_ok, 1)

            def residual(b):
                dve.wait_ge(ao_ok, b + 1)
                dve.wait_ge(xb_ok, b + 1)
                dve.tensor_tensor(x1_s[:, b, :], banks[AO][0:S, 0:D], x_s[:, b, :], ALU.add).then_inc(x1_ok, 1)
                dve.wait_ge(x1_ok, b + 1)
                row_stats(1, b)

            def a_slot(b):
                if 0 <= b - 1 < B:
                    shift_low(b - 1)
                if b < B:
                    row_max(b, 0)
                if 0 <= b - 3 < B:
                    divide(b - 3)
                if b < B:
                    for g in range(1, NG):
                        row_max(b, g)
                if 0 <= b - 3 < B:
                    residual(b - 3)

            def norm_rows(b):
                after(dve, xtp_ok, b)
                normalize(xr_s[:], 1, b, xr_ok)

            def x_slot(b):
                if b < B:
                    dve.wait_ge(s2_ok, b + 1)
                    after(dve, e2_ok, b)
                    dve.scalar_tensor_tensor(sc_s[:], banks[SC][0:S, 0:S2], D ** -0.5, mask_s[:],
                                             ALU.mult, ALU.add).then_inc(sc_ok, 1)
                    dve.wait_ge(sc_ok, b + 1)
                    dve.tensor_reduce(red_s[:, 0:1], sc_s[:], AX.X, ALU.max, negate=True).then_inc(nm2_ok, 1)
                if b + 2 < B:
                    norm_rows(b + 2)
                if b < B:
                    dve.wait_ge(e2_ok, b + 1)
                    after(dve, y_ok, b - 1)
                    dve.reciprocal(rec2_s[:, b % 2:b % 2 + 1], red_s[:, 1:2]).then_inc(r2_ok, 1)
                if 0 <= b - 2 < B:
                    dve.wait_ge(co_ok, b - 1)
                    dve.tensor_tensor(x1_s[:, b - 2, :], banks[CO][0:S, 0:D], x1_s[:, b - 2, :], ALU.add).then_inc(x2_ok, 1)
                    dve.wait_ge(x2_ok, b - 1)
                    row_stats(2, b - 2)

            def ffn_norm(h):
                inverse_root(2, h)
                for b in range(HB * h, HB * h + HB):
                    normalize(xn_s[:, b, :], 2, b, xn_ok)

            def ffn_in(h):
                for k in range(KD):
                    dve.wait_ge(x3h_ok, KD * h + k + 1)
                    dve.tensor_tensor(xl_t[:, k, HT * h:HT * h + HT], banks[k][:, 0:HT],
                                      xh_t[:, k, HT * h:HT * h + HT].bitcast(F32), ALU.subtract).then_inc(x3l_ok, 1)

            def ffn_hidden(h, f):
                n = FB * h + f
                toks = slice(HT * h, HT * h + HT)
                dve.wait_ge(h_ok, n + 1)
                dve.tensor_copy(hh_s[:, f, toks], h_s[:, n % 2, :]).then_inc(hh_ok, 1)
                dve.wait_ge(hh_ok, n + 1)
                dve.tensor_tensor(hl_s[:, f, toks], h_s[:, n % 2, :], hh_s[:, f, toks].bitcast(F32),
                                  ALU.subtract).then_inc(hl_ok, 1)

            def ffn_out(b):
                dve.wait_ge(f_ok, b + 1)
                dve.wait_ge(xb2_ok, b + 1)
                dve.tensor_tensor(x_s[:, b, :], banks[OUT[b % 4]][0:S, 0:D], x_s[:, b, :], ALU.add).then_inc(y2_ok, 1)

            for b in range(B):
                a_slot(b)
                if b in (1, 2):
                    weight_sum(0, b - 1)
                if b in (3, 4):
                    weight_sum(1, b - 3)
                if b == 5:
                    thresholds()
            inverse_root(1, 0)
            norm_rows(0)
            a_slot(B)
            norm_rows(1)
            a_slot(B + 1)
            a_slot(B + 2)
            inverse_root(1, 1)
            for b in range(B + 2):
                if b == HB + 2:
                    dve.wait_ge(xnp_ok, 4)
                    ffn_norm(0)
                x_slot(b)
                if b == B:
                    ffn_in(0)
            ffn_norm(1)
            for f in range(FB):
                ffn_hidden(0, f)
            ffn_in(1)
            for f in range(FB):
                ffn_hidden(1, f)
                if f % 2:
                    ffn_out(f // 2)
            for b in range(HB, B):
                ffn_out(b)

        @block.tensor
        def _(pe):
            def rows_to_columns(h, first, signal):
                for k in range(KD):
                    for i in range(HB):
                        pe.wait_ge(xn_ok, first + HB * h + i + 1)
                        mm = pe.transpose(banks[k][:, S * i:S * i + S],
                                          xn_s[:, HB * h + i, P * k:P * k + P], eye_s[0:S, 0:S])
                    mm.then_inc(signal, 1)

            def split_over_k(out, lhs, rhs):
                for k in range(KD):
                    mm = pe.matmul(out, lhs(k), rhs(k), start=(k == 0), stop=(k == KD - 1))
                return mm

            pe.wait_ge(ld_eye, 16)
            for h in range(HALVES):
                after(pe, xnt_ok, KD * h)
                rows_to_columns(h, 0, xnp_ok)
                if h == 0:
                    pe.wait_ge(ld_qk, 32)
                pe.wait_ge(xnt_ok, KD * h + KD)
                for m in range(4):
                    n = 4 * h + m
                    after(pe, r1_ok, n - 1)
                    split_over_k(banks[2 + n % 2][:, 0:HT], lambda k: wqkv_s[:, k, P * m:P * m + P],
                                 lambda k: xn_t[:, k, HT * h:HT * h + HT]).then_inc(qkp_ok, 1)
            pe.wait_ge(ld_v, 32)
            for b in range(B):
                after(pe, v_ok, b - 1)
                split_over_k(banks[V0 + b % 2][0:S, 0:D], lambda k: xn_t[:, k, S * b:S * b + S],
                             lambda k: wqkv_s[:, k, 2 * D:3 * D]).then_inc(vp_ok, 1)
            pe.wait_ge(ld_wx, 64)
            for m in range(KD):
                split_over_k(banks[6 + m][:, 0:D], lambda k: wq_s[:, k, P * m:P * m + P],
                             lambda k: wk_s[:, k, :]).then_inc(wa_p, 1)

            def masked_scores(bank, mask, left, right, toks, g, deep, signal):
                s = banks[bank][0:S, 0:GH * S]
                pe.matmul(s, eyeb_s[0:S, 0:S], mask[:].unsqueeze(1).to_broadcast([S, GH, S]), start=True, stop=False)
                for i in range(GH):
                    mm = pe.matmul(s[:, S * i:S * i + S], left[0:deep, GH * g + i, toks], right[0:deep, GH * g + i, toks],
                                   start=False, stop=(i == GH - 1))
                mm.then_inc(signal, 1)

            def scores(b, g):
                after(pe, max_ok, NG * b + g - 1)
                masked_scores(g % 2, band_s, q_st, k_st, slice(S * b, S * b + S), g, QK, s_ok)

            def scores_t(b, g):
                if g == 0:
                    pe.wait_ge(shift_ld, 32 * (b + 1))
                after(pe, exp_ok, NG * b + g - 1)
                masked_scores(2 + g % 2, bandt_s, k_st, q_st, slice(S * b, S * b + S), g, QKM, st_p)

            def values(b, g):
                pe.wait_ge(exp_ok, NG * b + g + 1)
                if g == 0:
                    after(pe, ov_ok, b)
                for i in range(GH):
                    mm = pe.matmul(banks[OV][QUAD * i:QUAD * i + DH + 1, S * g:S * g + S], v_s[:, b, GH * g + i, :],
                                   pt_s[:, g % 2, i, :], start=True, stop=True)
                mm.then_inc(pv_ok, 1)

            def values_to_rows(b):
                pe.wait_ge(ov_ok, b + 1)
                after(pe, o_ok, b)
                for g in range(NG):
                    mm = pe.transpose(banks[OP][0:S, P * g:P * g + P], ov_s[:, g, :], eye_s[:])
                mm.then_inc(op_ok, 1)

            def heads_to_columns(b):
                pe.wait_ge(o_ok, b + 1)
                pe.wait_ge(sl_ok, min(B, b + 3))
                for k in range(KD):
                    mm = pe.transpose(banks[SMALL][:, S * k:S * k + S], o_s[:, P * k:P * k + P], eye_s[0:S, 0:S])
                mm.then_inc(otp_ok, 1)

            def max_to_columns(b):
                pe.wait_ge(max_ok, NG * b + NG)
                after(pe, sl_ok, b)
                after(pe, ot_ok, b - 2)
                pe.transpose(banks[SMALL][0:NH, 0:S], nmax[:], eye_s[0:S, 0:S]).then_inc(mt_ok, 1)

            def project(b):
                pe.wait_ge(ot_ok, b + 1)
                after(pe, x1_ok, b)
                split_over_k(banks[AO][0:S, 0:D], lambda k: ot_s[:, k, :], lambda k: wout_s[:, k, :]).then_inc(ao_ok, 1)

            def a_slot(b):
                for g in range(NG):
                    if b < B:
                        scores(b, g)
                    if 0 <= b - 2 < B:
                        scores_t(b - 2, g)
                        if g:
                            values(b - 2, g - 1)
                    if 0 <= b - 3 < B:
                        if g == 0:
                            values_to_rows(b - 3)
                        if g == 1:
                            heads_to_columns(b - 3)
                        if g == 3:
                            project(b - 3)
                if 0 <= b - 2 < B:
                    values(b - 2, NG - 1)
                if b < B:
                    max_to_columns(b)

            def norm_to_columns(b):
                pe.wait_ge(xr_ok, b + 1)
                after(pe, xt_ok, b)
                for k in range(KD):
                    mm = pe.transpose(banks[XT][:, S * k:S * k + S], xr_s[:, P * k:P * k + P], eye_s[0:S, 0:S])
                mm.then_inc(xtp_ok, 1)

            def queries(b):
                pe.wait_ge(xt_ok, b + 1)
                after(pe, tt_ok, b)
                for m in range(KD):
                    mm = split_over_k(banks[TT][:, S * m:S * m + S], lambda k: wa_s[:, k, P * m:P * m + P],
                                      lambda k: xt_s[:, k, :])
                mm.then_inc(ttp_ok, 1)

            def x_slot(b):
                if 0 <= b - 1 < B:
                    pe.wait_ge(e2_ok, b)
                    after(pe, pt_ok, b - 1)
                    for c in range(CC):
                        mm = pe.transpose(banks[PT][0:CP, S * c:S * c + S], p2_s[:, CP * c:CP * c + CP], eye_s[0:S, 0:S])
                    mm.then_inc(ptp_ok, 1)
                if b < B:
                    pe.wait_ge(tt_ok, b + 1)
                    after(pe, sc_ok, b)
                    split_over_k(banks[SC][0:S, 0:S2], lambda k: tt_s[:, k, :],
                                 lambda k: ctx_t[:, k, S2 * b:S2 * b + S2]).then_inc(s2_ok, 1)
                if b + 1 < B:
                    norm_to_columns(b + 1)
                if 0 <= b - 1 < B:
                    pe.wait_ge(pt_ok, b)
                    after(pe, y_ok, b - 1)
                    for c in range(CC):
                        mm = pe.matmul(banks[YY][0:S, 0:D], p2t_s[:, c, :], ctx_r[:, (b - 1) * CC + c, :],
                                       start=(c == 0), stop=(c == CC - 1))
                    mm.then_inc(yp_ok, 1)
                if b + 1 < B:
                    queries(b + 1)
                if 0 <= b - 2 < B:
                    pe.wait_ge(yt_ok, b - 1)
                    after(pe, x2_ok, b - 2)
                    split_over_k(banks[CO][0:S, 0:D], lambda k: yt_s[:, k, :], lambda k: wvt_s[:, k, :]).then_inc(co_ok, 1)
                if 0 <= b - 1 < B:
                    pe.wait_ge(y_ok, b)
                    after(pe, yt_ok, b - 1)
                    for k in range(KD):
                        mm = pe.transpose(banks[YT][:, S * k:S * k + S], y_s[:, P * k:P * k + P], eye_s[0:S, 0:S])
                    mm.then_inc(ytp_ok, 1)

            def ffn_in(h):
                after(pe, x3l_ok, KD * h)
                rows_to_columns(h, B, x3p_ok)

            def ffn_hidden(h, f):
                n = FB * h + f
                if f == 0:
                    pe.wait_ge(x3l_ok, KD * h + KD)
                after(pe, h_ok, n - 1)
                for k in range(KD):
                    for j, part in enumerate((xh_t, xl_t)):
                        mm = pe.matmul(banks[HID[n % 2]][:, 0:HT], w1_r[:, k, P * f:P * f + P],
                                       part[:, k, HT * h:HT * h + HT], start=(k == 0 and j == 0),
                                       stop=(k == KD - 1 and j == 1))
                mm.then_inc(hp_ok, 1)

            def ffn_out(b):
                after(pe, y2_ok, b - 3)
                for f in range(FB):
                    pe.wait_ge(hl_ok, FB * (b // HB) + f + 1)
                    for j, part in enumerate((hh_s, hl_s)):
                        mm = pe.matmul(banks[OUT[b % 4]][0:S, 0:D], part[:, f, S * b:S * b + S], w2_r[:, f, :],
                                       start=(f == 0 and j == 0), stop=(f == FB - 1 and j == 1))
                mm.then_inc(f_ok, 1)

            pe.wait_ge(ld_c, 16 * 7)
            pe.wait_ge(vones_ok, 1)
            pe.wait_ge(kones_ok, 16)
            pe.wait_ge(ovz_ok, 1)
            pe.wait_ge(r1_ok, 8)
            pe.wait_ge(wa_ok, KD)
            for b in range(B + 1):
                if b % HB == 0 and b < B:
                    pe.wait_ge(qk_ld[b // HB], 16 * (len(Q_RUNS) + len(K_RUNS)))
                if b == 6:
                    pe.wait_ge(thr_ok, 4)
                a_slot(b)
                if b == 5:
                    pe.wait_ge(ws_ok, 4)
                    pe.wait_ge(ones_ok, 1)
                    pe.wait_ge(x1_ok, 3)
                    pe.matmul(banks[AO][:, 0:4], ones_s[:], wsum[:].rearrange("p a b -> p (a b)"),
                              start=True, stop=True).then_inc(wsp_ok, 1)
            norm_to_columns(0)
            a_slot(B + 1)
            queries(0)
            pe.wait_ge(ld_ctx, 64)
            a_slot(B + 2)
            for b in range(B + 2):
                if b == B:
                    ffn_in(0)
                x_slot(b)
            pe.wait_ge(tern_ok, 2 * KD * F // TC)
            for f in range(FB):
                ffn_hidden(0, f)
            ffn_in(1)
            for f in range(FB):
                ffn_hidden(1, f)
                if f % 2:
                    ffn_out(f // 2)
            for b in range(HB, B):
                ffn_out(b)


def kernel(**inputs):
    import numpy as np
    import concourse.bacc as bacc
    from concourse.bass_utils import run_bass_kernel_spmd as run

    def rows(a):
        return np.ascontiguousarray(a)

    order = np.array([side * D + (2 * g + k) * DH + d
                      for side in range(2) for k in range(2) for d in range(DH) for g in range(NH // 2)])
    w_qkv = np.asarray(inputs["L0_attn_w_qkv"])
    b_qkv = np.asarray(inputs["L0_attn_b_qkv"])
    i, j = np.arange(S)[:, None], np.arange(S)[None, :]
    allowed = (j % STRIDE == 0) | (np.abs(i - j) <= WINDOW)
    bf16 = mybir.dt.np(BF16)
    band = np.where(allowed, 0.0, BIG).astype(bf16)
    ctx = np.asarray(inputs["ctx_1024"]).reshape(B * S2, D)
    arrays = {
        "x": rows(inputs["x"]),
        "ctx_rows": rows(ctx),
        "ctx_cols": rows(ctx.T),
        "mask": rows(inputs["mask_SxS2_ik0"]),
        "w_qkv": rows(np.concatenate([w_qkv[:, order], w_qkv[:, 2 * D:]], axis=1)),
        "b_qk": rows(b_qkv[order].reshape(4, P).T),
        "b_v": rows(b_qkv[2 * D:]),
        "w_out": rows(inputs["L0_attn_w_out"]),
        "b_out": rows(inputs["L0_attn_b_out"]),
        "wq": rows(inputs["L0_xattn_Wq"]),
        "wk": rows(inputs["L0_xattn_Wk"]),
        "wv_t": rows(np.asarray(inputs["L0_xattn_Wv"]).T),
        "w1_t": rows(np.asarray(inputs["L0_ffn_W1"]).T),
        "b1": rows(np.asarray(inputs["L0_ffn_b1"]).reshape(FB, P).T),
        "w2_t": rows(np.asarray(inputs["L0_ffn_W2"]).T),
        "b2": rows(inputs["L0_ffn_b2"]),
        "eye": np.eye(P, dtype=np.float32),
        "eye_b": np.eye(P).astype(bf16),
        "k_ones": np.ones((QKM - QK, NH * T), dtype=bf16),
        "band": band,
        "band_t": rows(band.T),
    }
    nc = bacc.Bacc("TRN2", target_bir_lowering=False, num_devices=1)
    aps = {name: nc.dram_tensor(name, a.shape, mybir.dt.from_np(a.dtype), kind="ExternalInput").ap()
           for name, a in arrays.items()}
    out = nc.dram_tensor("out", (B, S, D), F32, kind="ExternalOutput").ap()
    build(nc, out=out, **aps)
    return run(nc, [arrays], core_ids=[0]).results[0]["out"]
```

```python
from contextlib import ExitStack

import concourse.bass as bass
from concourse import mybir

ALU = mybir.AluOpType
ACT = mybir.ActivationFunctionType
AX = mybir.AxisListType
F32 = mybir.dt.float32
F32R = mybir.dt.float32r
BF16 = mybir.dt.bfloat16
I32 = mybir.dt.int32

B, S, D = 8, 112, 256
T = B * S
P = 128
KD = D // P
NH, DH = 16, 16
S2 = 375
CC, CP = 3, 125
F = 1024
FB = F // P
TC = 512
HALVES = 2
HB = B // HALVES
HT = HB * S
NG, GH = 4, 4
QUAD = 32
WARM, WARM_GAP = 30, 6
EDGE = S - 1 - 64
MAGIC = 0x5F3759DF
STRIDE, WINDOW = 32, 64
EPS = 1e-5
BIG = -1.0e30
PARTS = 3
QK = 6 * DH
QKM = QK + 2
Q_RUNS = [(0, 0, 3), (3, 0, 2), (5, 0, 1)]
K_RUNS = [(0, 0, 3), (3, 1, 2), (5, 2, 1)]


def build(nc, x, ctx_rows, ctx_cols, mask, w_qkv, b_qk, b_v, w_out, b_out, wq, wk, wv_t,
          w1_t, b1, w2_t, b2, eye, eye_b, k_ones, band, band_t, out):
    with ExitStack() as stack:
        def sb(name, shape, dt=F32, where=stack):
            return where.enter_context(nc.sbuf_tensor(name, shape, dt))

        def bank(name):
            return stack.enter_context(nc.psum_tensor(name, [P, 512], F32))

        def sem(name):
            return stack.enter_context(nc.semaphore(name))

        with ExitStack() as whole:
            wout_s = sb("wout_s", [P, KD, D], F32, whole)
            wq_s = sb("wq_s", [P, KD, D], F32, whole)
            wk_s = sb("wk_s", [P, KD, D], F32, whole)
        wvt_h = sb("wvt_h", [P, KD, D], F32R)
        wout_h = sb("wout_h", [P, KD, D], F32R)
        wout_l = sb("wout_l", [P, KD, D], F32R)
        wvt_s = sb("wvt_s", [P, KD, D])
        wa_s = sb("wa_s", [P, KD, D])
        bqk_s = sb("bqk_s", [P, 4])
        bv_s = sb("bv_s", [S, D])
        bout_s = sb("bout_s", [S, D])
        b1_s = sb("b1_s", [P, FB])
        b2_s = sb("b2_s", [S, D])
        eye_s = sb("eye_s", [P, P])
        eyeb_s = sb("eyeb_s", [P, P], BF16)
        band_s = sb("band_s", [S, S], BF16)
        bandt_s = sb("bandt_s", [S, S], BF16)
        ones_s = sb("ones_s", [P, P])
        mask_i = sb("mask_i", [S, S2], I32)
        mask_s = mask_i[:].bitcast(F32)
        x_s = sb("x_s", [S, B, D])
        x1_s = sb("x1_s", [S, B, D])
        with ExitStack() as rows:
            xn_s = sb("xn_s", [S, B, D], F32, rows)
        xn_room = sb("xn_room", [S, B - 2, D])
        wvt_l = sb("wvt_l", [P, KD, D], F32R)
        stats = sb("stats", [S, 3, B, 6])
        mv = sb("mv", [S, 3, B, 2])
        var = sb("var", [S, 3, B])
        root = sb("root", [S, 3, 4, B])
        gelu_s = sb("gelu_s", [P, 1])
        tmp = sb("tmp", [S, 2, B])
        v_s = sb("v_s", [S, B, NH, DH + 1])
        nmax = sb("nmax", [S, 2, NH])
        shift = sb("shift", [NH, 2, S], BF16)
        pt_s = sb("pt_s", [S, 2, GH, S])
        ov_s = sb("ov_s", [P, NG, S])
        rec_s = sb("rec_s", [S, NH])
        o_s = sb("o_s", [S, D])
        ot_h = sb("ot_h", [P, KD, S], F32R)
        ot_l = sb("ot_l", [P, KD, S], F32R)
        xt_s = sb("xt_s", [P, KD, S])
        tt_s = sb("tt_s", [P, KD, S])
        red_s = sb("red_s", [S, 2])
        rec2_s = sb("rec2_s", [S, 2])
        p2t_s = sb("p2t_s", [CP, CC, S])
        yt_h = sb("yt_h", [P, KD, S], F32R)
        yt_l = sb("yt_l", [P, KD, S], F32R)
        w1_s = sb("w1_s", [P, KD, F])
        w2_s = sb("w2_s", [P, FB, D])
        w1_r = sb("w1_r", [P, KD, F], F32R)
        w2_r = sb("w2_r", [P, FB, D], F32R)
        wsum = sb("wsum", [P, 2, 4])
        thr = sb("thr", [P, 3, 2])
        low_s = sb("low_s", [P, 2, TC])

        with ExitStack() as first:
            wqkv_s = sb("wqkv_s", [P, KD, 3 * D], F32, first)
            wh_s = sb("wh_s", [P, KD, 3 * D], F32R, first)
            part_s = sb("part_s", [P, 4, PARTS, HT], BF16, first)
            rest_s = sb("rest_s", [P, 2, HT], F32, first)
        ctx_r = sb("ctx_r", [CP, B * CC, D])
        sc_s = sb("sc_s", [S, S2])
        p2_s = sb("p2_s", [S, S2])
        xr_s = sb("xr_s", [S, D])

        with ExitStack() as early:
            q_st = sb("q_st", [QKM, NH, T], BF16, early)
            k_st = sb("k_st", [QKM, NH, T], BF16, early)
            with ExitStack() as proj:
                wl_s = sb("wl_s", [P, KD, 3 * D], F32R, proj)
                xnh_t = sb("xnh_t", [P, KD, T], F32R, proj)
                xnl_t = sb("xnl_t", [P, KD, T], F32R, proj)
            ctx_t = sb("ctx_t", [P, KD, B * S2], F32, early)
        xh_t = sb("xh_t", [P, KD, T], F32R)
        xl_t = sb("xl_t", [P, KD, T], F32R)
        h_s = sb("h_s", [P, 4, HT])
        hh_s = sb("hh_s", [P, FB, T], F32R)
        hl_s = sb("hl_s", [P, FB, T], F32R)

        parts_d = nc.dram_tensor("parts_d", (2, PARTS, P, 2, T), BF16, kind="Internal").ap()

        banks = [bank(f"bank{i}") for i in range(8)]

        def sems(names):
            return [sem(n) for n in names.split()]

        ld_eye, ld_x0, ld_x1, ld_qk, ld_v, ld_c, ld_wx = sems("ld_eye ld_x0 ld_x1 ld_qk ld_v ld_c ld_wx")
        ld_x = [ld_x0, ld_x1]
        ld_ctxt, ld_ctxr = sems("ld_ctxt0 ld_ctxt1 ld_ctxt2 ld_ctxt3"), sems("ld_ctxr0 ld_ctxr1 ld_ctxr2 ld_ctxr3")
        ld_w = sems("ld_w1 ld_w2")
        warm_ok, ones_ok, vones_ok, kones_ok, mask_ok, ovz_ok = sems("warm_ok ones_ok vones_ok kones_ok mask_ok ovz_ok")
        st_ok, mv_ok, var_ok, root_ok, xn_ok = sems("st_ok mv_ok var_ok root_ok xn_ok")
        wh_ok, wl_ok, xnl_ok = sems("wh_ok wl_ok xnl_ok")
        xnp_ok, xnt_ok, qkp_ok, p1_ok, r1_ok, p2_ok, p3_ok, vp_ok, v_ok, xb_ok = sems(
            "xnp_ok xnt_ok qkp_ok p1_ok r1_ok p2_ok p3_ok vp_ok v_ok xb_ok")
        pw_ok = sems("pw_ok0 pw_ok1 pw_ok2 pw_ok3")
        qk_ld = sems("qk_ld0 qk_ld1")
        wa_p, wa_ok, ws_ok, wsp_ok, thr_sum, thr_mean, thr_ok, low_ok, tern_ok = sems(
            "wa_p wa_ok ws_ok wsp_ok thr_sum thr_mean thr_ok low_ok tern_ok")
        s_ok, max_ok, mt_ok, sh_ok, sl_ok, shift_ld = sems("s_ok max_ok mt_ok sh_ok sl_ok shift_ld")
        woh_ok, wol_ok, otl_ok, ytl_ok = sems("woh_ok wol_ok otl_ok ytl_ok")
        st_p, exp_ok, pv_ok, ov_ok, op_ok, rec_ok, o_ok, otp_ok, ot_ok, ao_ok, x1_ok = sems(
            "st_p exp_ok pv_ok ov_ok op_ok rec_ok o_ok otp_ok ot_ok ao_ok x1_ok")
        xr_ok, xtp_ok, xt_ok, ttp_ok, tt_ok, s2_ok, sc_ok, nm2_ok, e2_ok, r2_ok = sems(
            "xr_ok xtp_ok xt_ok ttp_ok tt_ok s2_ok sc_ok nm2_ok e2_ok r2_ok")
        ptp_ok, pt_ok, yp_ok, yt_ok, co_ok, x2_ok = sems(
            "ptp_ok pt_ok yp_ok yt_ok co_ok x2_ok")
        x3p_ok, x3h_ok, x3l_ok, hp_ok, h_ok, hh_ok, hho_ok, hl_ok, hlp_ok, f_ok, y2_ok, xb2_ok, st_out = sems(
            "x3p_ok x3h_ok x3l_ok hp_ok h_ok hh_ok hho_ok hl_ok hlp_ok f_ok y2_ok xb2_ok st_out")

        warm_s = x1_s[:, 0, :].bitcast(BF16)[:, 0:HT]

        def by_vector(n):
            return n in VECTOR_HIGH

        def wait_high(eng, n):
            before = sum(m < n for m in VECTOR_HIGH)
            if by_vector(n):
                eng.wait_ge(hho_ok, before + 1)
            else:
                eng.wait_ge(hh_ok, n + 1 - before)

        def wait_low(eng, n):
            if n in POOL_LOW:
                eng.wait_ge(hlp_ok, POOL_LOW.index(n) + 1)
            else:
                eng.wait_ge(hl_ok, n + 1 - sum(m < n for m in POOL_LOW))

        def after(eng, signal, count):
            if count > 0:
                eng.wait_ge(signal, count)

        V0, OV, OP, SMALL, AO = 4, 4, 5, 6, 7
        XT, TT, SC, YY, PT, CO = 0, 0, 1, 2, 3, 5
        HID = (6, 7)

        def score_bank(b, g):
            return g % 2 if b >= 2 else g

        HIDDEN_BANK = [HID[f % 2] for f in range(FB)] + [(*HID, CO)[f % 3] for f in range(FB)]
        QK_BANK = (2, 3, 6, 7)
        VECTOR_HIGH = (6, 9, 11, 13, 15)
        SUM_STEPS = [(4, 2), (4, 3), (5, 1), (5, 2), (5, 3), (6, 1), (6, 2), (6, 3)]
        POOL_LOW = (2, 4)
        OUT = (4, 0, 1, 3)

        block = stack.enter_context(nc.Block())

        @block.sync
        def _(sp):
            for h in range(HALVES):
                sp.dma_start(x_s[:, HB * h:HB * h + HB, :],
                             x[HB * h:HB * h + HB].rearrange("b s d -> s b d")).then_inc(ld_x[h], 16)
                if h == 0:
                    sp.dma_start(wqkv_s[:, :, 0:2 * D],
                                 w_qkv[:, 0:2 * D].rearrange("(k p) e -> p k e", p=P)).then_inc(ld_qk, 16)
                    sp.dma_start(bqk_s[:], b_qk).then_inc(ld_qk, 16)
            sp.dma_start(wqkv_s[:, :, 2 * D:3 * D],
                         w_qkv[:, 2 * D:3 * D].rearrange("(k p) e -> p k e", p=P)).then_inc(ld_v, 16)
            sp.dma_start(bv_s[:], b_v.partition_broadcast(S)).then_inc(ld_v, 16)
            for dst, src in ((eyeb_s, eye_b), (band_s, band), (bandt_s, band_t), (mask_i, mask),
                             (bout_s, b_out.partition_broadcast(S)), (b2_s, b2.partition_broadcast(S)), (b1_s, b1)):
                sp.dma_start(dst[:], src).then_inc(ld_c, 16)
            sp.dma_start(k_st[QK:QKM].rearrange("p h t -> p (h t)"), k_ones).then_inc(kones_ok, 16)
            for w, src in ((wq_s, wq), (wk_s, wk), (wvt_s, wv_t), (wout_s, w_out)):
                sp.dma_start(w[:], src.rearrange("(k p) e -> p k e", p=P)).then_inc(ld_wx, 16)
            def stack_parts(h, side, i):
                for m in (2 * side, 2 * side + 1):
                    sp.wait_ge(pw_ok[m], 16 * (h + 1))
                dst, runs = ((q_st, Q_RUNS), (k_st, K_RUNS))[side]
                row, part, count = runs[i]
                toks = slice(HT * h, HT * h + HT)
                if side == 0:
                    src = parts_d[0, part:part + count, :, :, toks].rearrange("c (d g) k t -> (c d) (g k) t", d=DH)
                else:
                    src = parts_d[1, part, :, :, toks].rearrange(
                        "(d g) k t -> d (g k) t", d=DH).unsqueeze(0).to_broadcast([count, DH, NH, HT])
                sp.dma_start(dst[DH * row:DH * (row + count), :, toks], src).then_inc(qk_ld[h], 16)

            def parts_to_dram(n):
                h, m = n // 4, n % 4
                sp.wait_ge(p3_ok, n + 1)
                sp.dma_start(parts_d[m // 2, :, :, m % 2, HT * h:HT * h + HT].rearrange("c p t -> p c t"),
                             part_s[:, m]).then_inc(pw_ok[m], 16)

            for n in range(4):
                parts_to_dram(n)
            for side in range(2):
                for i in range(3):
                    stack_parts(0, side, i)
            for n in range(4, 8):
                parts_to_dram(n)
            for b in range(B):
                sp.wait_ge(sl_ok, b + 1)
                for r in range(2):
                    sp.dma_start(q_st[QK + r:QK + r + 1, :, S * b:S * b + S],
                                 shift[:, r, :]).then_inc(shift_ld, 16)
                for side, i in (((0, 0), (0, 1)), ((0, 2), (1, 0), (1, 1)), ((1, 2),))[b] if b < 3 else ():
                    stack_parts(1, side, i)
            for b in range(B):
                sp.wait_ge(y2_ok, b + 1)
                sp.dma_start(out[b], x_s[:, b, :]).then_inc(st_out, 16)
            sp.wait_ge(st_out, 16 * B)

        @block.gpsimd
        def _(pool):
            def ternary(i):
                pool.wait_ge(thr_ok, 2)
                w, t = ((w1_s, w1_r), (w2_s, w2_r))[i]
                wf = w[:].rearrange("p a b -> p (a b)")
                tf = t[:].rearrange("p a b -> p (a b)")
                for c in range(KD * F // TC):
                    n = KD * F // TC * i + c
                    sl = slice(TC * c, TC * c + TC)
                    after(pool, tern_ok, n - 1)
                    pool.tensor_scalar(low_s[:, c % 2, :], wf[:, sl], thr[:, 2, i:i + 1], None, ALU.is_lt).then_inc(low_ok, 1)
                    pool.tensor_scalar(wf[:, sl], wf[:, sl], thr[:, 1, i:i + 1], None, ALU.is_gt).then_inc(low_ok, 1)
                    pool.wait_ge(low_ok, 2 * n + 2)
                    pool.tensor_tensor(tf[:, sl], wf[:, sl], low_s[:, c % 2, :], ALU.subtract).then_inc(tern_ok, 1)

            pool.memset(warm_s, 0.0).then_inc(warm_ok, 1)
            pool.dma_start(eye_s[:], eye).then_inc(ld_eye, 16)
            for c in range(5):
                cols = slice(P * c, P * c + P) if c < 4 else slice(2 * D, 3 * D)
                pool.wait_ge(wh_ok, c + 1)
                pool.tensor_tensor(wl_s[:, :, cols], wqkv_s[:, :, cols], wh_s[:, :, cols].bitcast(F32),
                                   ALU.subtract).then_inc(wl_ok, 1)
            for n in range(8):
                pool.wait_ge(p2_ok, n + 1)
                pool.tensor_tensor(part_s[:, n % 4, 2, :], rest_s[:, n % 2, :], part_s[:, n % 4, 1, :],
                                   ALU.subtract).then_inc(p3_ok, 1)
                if n == 0:
                    pool.memset(ones_s[:], 1.0).then_inc(ones_ok, 1)
                    pool.memset(v_s[:, :, :, DH:DH + 1], 1.0).then_inc(vones_ok, 1)
            pool.wait_ge(woh_ok, 1)
            pool.tensor_tensor(wout_l[:], wout_s[:], wout_h[:].bitcast(F32), ALU.subtract).then_inc(wol_ok, 1)
            pool.wait_ge(ld_c, 16 * 7)
            pool.wait_ge(xn_ok, B)
            for b in range(B):
                pool.tensor_tensor(x_s[:, b, :], x_s[:, b, :], bout_s[:], ALU.add).then_inc(xb_ok, 1)
            pool.wait_ge(woh_ok, 2)
            pool.wait_ge(xnp_ok, 2 * KD)
            pool.tensor_tensor(wvt_l[:], wvt_s[:], wvt_h[:].bitcast(F32), ALU.subtract).then_inc(wol_ok, 1)

            def ctx_cols_load(c):
                cols = slice(2 * S2 * c, 2 * S2 * (c + 1))
                pool.dma_start(ctx_t[:, :, cols], ctx_cols[:, cols].rearrange("(k p) t -> p k t", p=P)).then_inc(ld_ctxt[c], 16)

            def ctx_rows_load(c):
                rows = slice(2 * CC * c, 2 * CC * (c + 1))
                pool.dma_start(ctx_r[:, rows, :],
                               ctx_rows.rearrange("(c p) d -> p c d", p=CP)[:, rows, :]).then_inc(ld_ctxr[c], 16)

            pool.wait_ge(shift_ld, 32 * 3)
            for k in range(KD):
                pool.dma_start(w1_s[:, k, :], w1_t[P * k:P * k + P, :]).then_inc(ld_w[0], 16)
            pool.wait_ge(shift_ld, 32 * 4)
            for k in range(KD):
                pool.dma_start(w2_s[:, FB // 2 * k:FB // 2 * (k + 1), :],
                               w2_t.rearrange("(k p) d -> p k d", p=P)[:, FB // 2 * k:FB // 2 * (k + 1), :]).then_inc(ld_w[1], 16)
            pool.wait_ge(qk_ld[1], 16 * (len(Q_RUNS) + len(K_RUNS)))
            pool.wait_ge(qkp_ok, 8)
            pool.wait_ge(vp_ok, B)
            for b, load, c in ((4, ctx_cols_load, 0), (5, ctx_cols_load, 1), (6, ctx_rows_load, 0)):
                pool.wait_ge(shift_ld, 32 * (b + 1))
                load(c)
            pool.wait_ge(shift_ld, 32 * B)
            ctx_rows_load(1)
            ctx_cols_load(2)
            ctx_cols_load(3)
            ctx_rows_load(2)
            ctx_rows_load(3)
            pool.wait_ge(thr_sum, 1)
            pool.tensor_scalar(thr[:, 0, :], thr[:, 0, :], 1.0 / (F * D), 1e-8, ALU.mult, ALU.max).then_inc(thr_mean, 1)
            pool.wait_ge(thr_mean, 1)
            for j, c in ((1, 0.5), (2, -0.5)):
                pool.tensor_scalar(thr[:, j, :], thr[:, 0, :], c, None, ALU.mult).then_inc(thr_ok, 1)
            ternary(0)
            ternary(1)

            for b in range(B):
                if b == B - 1:
                    for n in POOL_LOW:
                        wait_high(pool, n)
                        pool.tensor_tensor(hl_s[:, n, 0:HT], h_s[:, n % 4, :], hh_s[:, n, 0:HT].bitcast(F32),
                                           ALU.subtract).then_inc(hlp_ok, 1)
                pool.wait_ge(x2_ok, b + 1)
                pool.tensor_tensor(x_s[:, b, :], x1_s[:, b, :], b2_s[:], ALU.add).then_inc(xb2_ok, 1)

        @block.scalar
        def _(act):
            def wide(n, at=0):
                return banks[n][:, at:at + KD * S].rearrange("p (k s) -> p k s", k=KD)

            def rows_out(h):
                for k in range(KD):
                    act.wait_ge(xnp_ok, KD * h + k + 1)
                    act.copy(xnh_t[:, k, HT * h:HT * h + HT], banks[k][:, 0:HT]).then_inc(xnt_ok, 1)

            def first_part(n):
                act.wait_ge(qkp_ok, n + 1)
                after(act, pw_ok[n % 4], 16 * (n // 4))
                act.activation(part_s[:, n % 4, 0, :], banks[QK_BANK[n % 4]][:, 0:HT], ACT.Identity,
                               bias=bqk_s[:, n % 4:n % 4 + 1]).then_inc(p1_ok, 1)

            def second_part(n):
                act.wait_ge(r1_ok, n + 1)
                act.copy(part_s[:, n % 4, 1, :], rest_s[:, n % 2, :]).then_inc(p2_ok, 1)

            for c in range(5):
                cols = slice(P * c, P * c + P) if c < 4 else slice(2 * D, 3 * D)
                act.wait_ge(*((ld_qk, 32) if c < 4 else (ld_v, 32)))
                act.copy(wh_s[:, :, cols], wqkv_s[:, :, cols]).then_inc(wh_ok, 1)
            rows_out(0)
            first_part(0)
            for n in range(1, 4):
                first_part(n)
                second_part(n - 1)
            second_part(3)
            rows_out(1)
            first_part(4)
            for n in range(5, 8):
                first_part(n)
                second_part(n - 1)
            second_part(7)
            for m in range(KD):
                act.wait_ge(wa_p, m + 1)
                act.copy(wa_s[:, m, :], banks[m][:, 0:D]).then_inc(wa_ok, 1)
            act.copy(wout_h[:], wout_s[:]).then_inc(woh_ok, 1)
            def shift_high(b):
                act.wait_ge(mt_ok, b + 1)
                after(act, shift_ld, 32 * b)
                act.copy(shift[:, 0, :], banks[SMALL][0:NH, 0:S]).then_inc(sh_ok, 1)

            def values_out(b):
                act.wait_ge(pv_ok, NG * b + NG)
                after(act, op_ok, b)
                act.copy(ov_s[:], banks[OV][:, 0:NG * S].rearrange("p (g s) -> p g s", g=NG)).then_inc(ov_ok, 1)

            def probs(b, g):
                n = NG * b + g
                act.wait_ge(st_p, n + 1)
                after(act, pv_ok, n - 1)
                act.activation(pt_s[:, g % 2, :, :],
                               banks[2 + g % 2][0:S, 0:GH * S].rearrange("p (h s) -> p h s", h=GH),
                               ACT.Exp, scale=DH ** -0.5).then_inc(exp_ok, 1)

            def heads_out(b):
                act.wait_ge(otp_ok, b + 1)
                after(act, ao_ok, b)
                act.copy(ot_h[:], wide(SMALL)).then_inc(ot_ok, 1)

            def a_slot(b):
                if 0 <= b - 1 < B:
                    shift_high(b - 1)
                if 0 <= b - 3 < B:
                    values_out(b - 3)
                if 0 <= b - 2 < B:
                    probs(b - 2, 0)
                    probs(b - 2, 1)
                if 0 <= b - 3 < B:
                    heads_out(b - 3)
                if b == 3:
                    act.wait_ge(wol_ok, 1)
                    act.copy(wvt_h[:], wvt_s[:]).then_inc(woh_ok, 1)
                if 0 <= b - 2 < B:
                    probs(b - 2, 2)
                    probs(b - 2, 3)

            def norm_out(b):
                act.wait_ge(xtp_ok, b + 1)
                after(act, ttp_ok, b)
                act.copy(xt_s[:], wide(XT)).then_inc(xt_ok, 1)

            def query_out(b):
                act.wait_ge(ttp_ok, b + 1)
                after(act, s2_ok, b)
                act.copy(tt_s[:], wide(TT, KD * S)).then_inc(tt_ok, 1)

            def cross_probs(b):
                act.wait_ge(nm2_ok, b + 1)
                after(act, ptp_ok, b)
                after(act, r2_ok, b)
                act.activation(p2_s[:], sc_s[:], ACT.Exp, bias=red_s[:, 0:1],
                               accum_out=red_s[:, 1:2]).then_inc(e2_ok, 1)

            def probs_out(b):
                act.wait_ge(ptp_ok, b + 1)
                after(act, yp_ok, b)
                act.copy(p2t_s[:], banks[PT][0:CP, 0:CC * S].rearrange("p (c s) -> p c s", c=CC)).then_inc(pt_ok, 1)

            def context_out(b):
                act.wait_ge(yp_ok, b + 1)
                after(act, co_ok, b)
                act.copy(yt_h[:], wide(YY)).then_inc(yt_ok, 1)

            def x_slot(b):
                if 0 <= b - 1 < B:
                    probs_out(b - 1)
                if b + 1 < B:
                    norm_out(b + 1)
                if b <= 3:
                    context_out(b - 1)
                cross_probs(b)
                if b > 3:
                    context_out(b - 1)
                if b + 1 < B:
                    query_out(b + 1)

            def ffn_in(h):
                for k in range(KD):
                    act.wait_ge(x3p_ok, KD * h + k + 1)
                    act.copy(xh_t[:, k, HT * h:HT * h + HT], banks[HID[k]][:, 0:HT]).then_inc(x3h_ok, 1)

            def ffn_hidden(h, f):
                n = FB * h + f
                act.wait_ge(hp_ok, n + 1)
                if n >= 4:
                    wait_low(act, n - 4)
                act.activation(h_s[:, n % 4, :], banks[HIDDEN_BANK[n]][:, 0:HT], ACT.Gelu,
                               bias=b1_s[:, f:f + 1]).then_inc(h_ok, 1)
                if f:
                    hidden_high(h, f - 1)
                if f == FB - 1:
                    hidden_high(h, f)

            def hidden_high(h, f):
                n = FB * h + f
                if not by_vector(n):
                    act.wait_ge(h_ok, n + 1)
                    act.copy(hh_s[:, f, HT * h:HT * h + HT], h_s[:, n % 4, :]).then_inc(hh_ok, 1)

            for b in range(B):
                a_slot(b)
            shift_high(B - 1)
            values_out(B - 3)
            probs(B - 2, 0)
            probs(B - 2, 1)
            heads_out(B - 3)
            norm_out(0)
            probs(B - 2, 2)
            probs(B - 2, 3)
            query_out(0)
            values_out(B - 2)
            probs(B - 1, 0)
            probs(B - 1, 1)
            norm_out(1)
            cross_probs(0)
            heads_out(B - 2)
            probs(B - 1, 2)
            query_out(1)
            probs(B - 1, 3)
            values_out(B - 1)
            probs_out(0)
            norm_out(2)
            context_out(0)
            heads_out(B - 1)
            cross_probs(1)
            query_out(2)
            for b in range(2, B - 1):
                x_slot(b)
            act.wait_ge(ld_c, 16 * 7)
            probs_out(B - 2)
            ffn_in(0)
            cross_probs(B - 1)
            context_out(B - 2)
            act.activation(gelu_s[:], b1_s[:, 0:1], ACT.Gelu)
            act.wait_ge(s2_ok, B)
            ffn_hidden(0, 0)
            probs_out(B - 1)
            ffn_hidden(0, 1)
            ffn_hidden(0, 2)
            context_out(B - 1)
            for f in range(3, FB):
                ffn_hidden(0, f)
            ffn_in(1)
            for f in range(FB):
                ffn_hidden(1, f)

        @block.vector
        def _(dve):
            def row_stats(n, b):
                dve.bn_stats(stats[:, n, b, :], (x_s if n == 0 else x1_s)[:, b, :]).then_inc(st_ok, 1)

            def root_guess(n, h):
                cols = slice(HB * h, HB * h + HB)
                call = HALVES * n + h
                dve.wait_ge(st_ok, HB * (call + 1))
                for b in range(HB * h, HB * h + HB):
                    dve.bn_aggr(mv[:, n, b, :], stats[:, n, b, :]).then_inc(mv_ok, 1)
                dve.wait_ge(mv_ok, HB * (call + 1))
                v = var[:, n, cols]
                dve.tensor_scalar(v, mv[:, n, cols, 1], EPS, None, ALU.add).then_inc(var_ok, 1)
                dve.wait_ge(var_ok, call + 1)
                dve.tensor_scalar(root[:, n, 0, cols].bitcast(I32), v.bitcast(I32), -0.5, float(MAGIC),
                                  ALU.mult, ALU.add).then_inc(root_ok, 1)

            def newton_step(n, h, i):
                cols = slice(HB * h, HB * h + HB)
                v, y, done = var[:, n, cols], root[:, n, i, cols], 10 * (HALVES * n + h) + 3 * i
                dve.wait_ge(root_ok, done + 1)
                dve.tensor_tensor(tmp[:, 0, cols], y, y, ALU.mult).then_inc(root_ok, 1)
                dve.wait_ge(root_ok, done + 2)
                dve.scalar_tensor_tensor(tmp[:, 1, cols], tmp[:, 0, cols], -0.5, v,
                                         ALU.mult, ALU.mult).then_inc(root_ok, 1)
                dve.wait_ge(root_ok, done + 3)
                dve.scalar_tensor_tensor(root[:, n, i + 1, cols], tmp[:, 1, cols], 1.5, y,
                                         ALU.add, ALU.mult).then_inc(root_ok, 1)

            def inverse_root(n, h):
                root_guess(n, h)
                for i in range(3):
                    newton_step(n, h, i)
                dve.wait_ge(root_ok, 10 * (HALVES * n + h + 1))

            def normalize(dst, n, b, signal):
                dve.tensor_scalar(dst, (x_s if n == 0 else x1_s)[:, b, :], mv[:, n, b, 0:1], root[:, n, 3, b:b + 1],
                                  ALU.subtract, ALU.mult).then_inc(signal, 1)

            def remainder(n):
                dve.wait_ge(p1_ok, n + 1)
                after(dve, p3_ok, n - 1)
                dve.scalar_tensor_tensor(rest_s[:, n % 2, :], banks[QK_BANK[n % 4]][:, 0:HT], bqk_s[:, n % 4:n % 4 + 1],
                                         part_s[:, n % 4, 0, :], ALU.add, ALU.subtract).then_inc(r1_ok, 1)

            def rows_low(h):
                for k in range(KD):
                    dve.wait_ge(xnt_ok, KD * h + k + 1)
                    dve.tensor_tensor(xnl_t[:, k, HT * h:HT * h + HT], banks[k][:, 0:HT],
                                      xnh_t[:, k, HT * h:HT * h + HT].bitcast(F32), ALU.subtract).then_inc(xnl_ok, 1)

            def add_value_bias(b):
                dve.wait_ge(ld_v, 32)
                dve.wait_ge(vp_ok, b + 1)
                dve.tensor_tensor(v_s[:, b, :, 0:DH],
                                  banks[V0 + b % 4][0:S, 0:D].rearrange("p (h d) -> p h d", h=NH),
                                  bv_s[:].rearrange("p (h d) -> p h d", h=NH), ALU.add).then_inc(v_ok, 1)

            dve.wait_ge(ld_x[0], 16)
            for b in range(HB):
                row_stats(0, b)
            inverse_root(0, 0)
            for b in range(HB):
                normalize(xn_s[:, b, :], 0, b, xn_ok)
            dve.wait_ge(ld_x[1], 16)
            for b in range(HB, B):
                row_stats(0, b)
            rows_low(0)
            root_guess(0, 1)
            newton_step(0, 1, 0)
            remainder(0)
            newton_step(0, 1, 1)
            remainder(1)
            newton_step(0, 1, 2)
            dve.wait_ge(root_ok, 10 * HALVES)
            normalize(xn_s[:, 4, :], 0, 4, xn_ok)
            normalize(xn_s[:, 5, :], 0, 5, xn_ok)
            remainder(2)
            normalize(xn_s[:, 6, :], 0, 6, xn_ok)
            normalize(xn_s[:, 7, :], 0, 7, xn_ok)
            remainder(3)
            add_value_bias(0)
            add_value_bias(1)
            rows_low(1)
            add_value_bias(2)
            add_value_bias(3)
            for n in range(4, 8):
                remainder(n)
            for b in range(HB, B):
                add_value_bias(b)

            def weight_sum(i, k):
                dve.wait_ge(ld_w[i], 32)
                n = KD * F // 4
                w = (w1_s, w2_s)[i]
                dve.tensor_reduce(wsum[:, i, k:k + 1], w[:].rearrange("p a b -> p (a b)")[:, n * k:n * k + n],
                                  AX.X, ALU.add, apply_absolute_value=True).then_inc(ws_ok, 1)

            def weight_totals():
                dve.wait_ge(wsp_ok, 1)
                dve.tensor_reduce(thr[:, 0, :], banks[AO][:, 0:8].rearrange("p (i k) -> p i k", k=4),
                                  AX.X, ALU.add).then_inc(thr_sum, 1)

            def low_part(low, high, bank_n, done, n, signal):
                dve.wait_ge(done, n + 1)
                dve.tensor_tensor(low[:], banks[bank_n][:, 0:KD * S].rearrange("p (k s) -> p k s", k=KD),
                                  high[:].bitcast(F32), ALU.subtract).then_inc(signal, 1)

            def cross_mask():
                dve.wait_ge(ld_c, 16 * 7)
                dve.tensor_scalar(mask_s, mask_i[:], 0.0, BIG, ALU.is_equal, ALU.mult).then_inc(mask_ok, 1)

            def shift_low(b):
                dve.wait_ge(sh_ok, b + 1)
                dve.tensor_tensor(shift[:, 1, :], banks[SMALL][0:NH, 0:S], shift[:, 0, :], ALU.subtract).then_inc(sl_ok, 1)

            def row_max(b, g):
                dve.wait_ge(s_ok, NG * b + g + 1)
                if g == 0:
                    after(dve, mt_ok, b - 1)
                dve.tensor_reduce(nmax[:, b % 2, GH * g:GH * g + GH],
                                  banks[score_bank(b, g)][0:S, 0:GH * S].rearrange("p (h s) -> p h s", h=GH),
                                  AX.X, ALU.max, negate=True).then_inc(max_ok, 1)

            def divide(b):
                dve.wait_ge(op_ok, b + 1)
                after(dve, otp_ok, b)
                o = banks[OP][0:S, :].rearrange("p (h d) -> p h d", d=QUAD)
                dve.reciprocal(rec_s[:], o[:, :, DH]).then_inc(rec_ok, 1)
                dve.wait_ge(rec_ok, b + 1)
                dve.tensor_tensor(o_s[:].rearrange("p (h d) -> p h d", h=NH), o[:, :, 0:DH],
                                  rec_s[:].unsqueeze(2).to_broadcast([S, NH, DH]), ALU.mult).then_inc(o_ok, 1)

            def heads_low(b):
                after(dve, ao_ok, b)
                low_part(ot_l, ot_h, SMALL, ot_ok, b, otl_ok)

            def context_low(b):
                after(dve, co_ok, b)
                low_part(yt_l, yt_h, YY, yt_ok, b, ytl_ok)

            def residual(b):
                dve.wait_ge(ao_ok, b + 1)
                dve.wait_ge(xb_ok, b + 1)
                dve.tensor_tensor(x1_s[:, b, :], banks[AO][0:S, 0:D], x_s[:, b, :], ALU.add).then_inc(x1_ok, 1)
                dve.wait_ge(x1_ok, b + 1)
                row_stats(1, b)

            def a_slot(b):
                if b >= 3:
                    shift_low(b - 1)
                row_max(b, 0)
                if 1 <= b < 3:
                    shift_low(b - 1)
                if 0 <= b - 3 < B:
                    divide(b - 3)
                if b < B:
                    for g in range(1, NG):
                        row_max(b, g)
                        if b >= 3 and g == 2:
                            heads_low(b - 3)
                        if (b, g) in SUM_STEPS:
                            weight_sum(*divmod(SUM_STEPS.index((b, g)), 4))
                        if b == B - 1:
                            if g == 1:
                                root_guess(1, 0)
                            if g == 3:
                                newton_step(1, 0, 0)
                                newton_step(1, 0, 1)
                                newton_step(1, 0, 2)
                if 0 <= b - 3 < B:
                    residual(b - 3)

            def norm_rows(b):
                after(dve, xtp_ok, b)
                normalize(xr_s[:], 1, b, xr_ok)

            def cross_max(b):
                dve.wait_ge(s2_ok, b + 1)
                after(dve, e2_ok, b)
                dve.scalar_tensor_tensor(sc_s[:], banks[SC][0:S, 0:S2], D ** -0.5, mask_s,
                                         ALU.mult, ALU.add).then_inc(sc_ok, 1)
                dve.wait_ge(sc_ok, b + 1)
                dve.tensor_reduce(red_s[:, 0:1], sc_s[:], AX.X, ALU.max, negate=True).then_inc(nm2_ok, 1)

            def cross_reciprocal(b):
                dve.wait_ge(e2_ok, b + 1)
                after(dve, x2_ok, b - 1)
                dve.reciprocal(rec2_s[:, b % 2:b % 2 + 1], red_s[:, 1:2]).then_inc(r2_ok, 1)

            def cross_residual(b):
                dve.wait_ge(co_ok, b + 1)
                dve.wait_ge(r2_ok, b + 1)
                dve.scalar_tensor_tensor(x1_s[:, b, :], banks[CO][0:S, 0:D], rec2_s[:, b % 2:b % 2 + 1],
                                         x1_s[:, b, :], ALU.mult, ALU.add).then_inc(x2_ok, 1)
                dve.wait_ge(x2_ok, b + 1)
                row_stats(2, b)

            def ffn_norm(b):
                dve.wait_ge(root_ok, 10 * (2 * HALVES + b // HB + 1))
                normalize(xn_s[:, b, :], 2, b, xn_ok)

            def ffn_in(h):
                for k in range(KD):
                    dve.wait_ge(x3h_ok, KD * h + k + 1)
                    dve.tensor_tensor(xl_t[:, k, HT * h:HT * h + HT], banks[HID[k]][:, 0:HT],
                                      xh_t[:, k, HT * h:HT * h + HT].bitcast(F32), ALU.subtract).then_inc(x3l_ok, 1)

            def ffn_hidden(h, f):
                n = FB * h + f
                toks = slice(HT * h, HT * h + HT)
                wait_high(dve, n)
                dve.tensor_tensor(hl_s[:, f, toks], h_s[:, n % 4, :], hh_s[:, f, toks].bitcast(F32),
                                  ALU.subtract).then_inc(hl_ok, 1)

            def ffn_high(h, f):
                n = FB * h + f
                dve.wait_ge(h_ok, n + 1)
                dve.tensor_copy(hh_s[:, f, HT * h:HT * h + HT], h_s[:, n % 4, :]).then_inc(hho_ok, 1)

            def ffn_out(b):
                dve.wait_ge(f_ok, b + 1)
                dve.wait_ge(xb2_ok, b + 1)
                dve.tensor_tensor(x_s[:, b, :], banks[OUT[b % 4]][0:S, 0:D], x_s[:, b, :], ALU.add).then_inc(y2_ok, 1)

            for b in range(B):
                a_slot(b)
            shift_low(B - 1)
            divide(B - 3)
            dve.wait_ge(root_ok, 10 * (HALVES + 1))
            norm_rows(0)
            cross_mask()
            weight_totals()
            norm_rows(1)
            heads_low(B - 3)
            residual(B - 3)
            divide(B - 2)
            cross_max(0)
            cross_reciprocal(0)
            norm_rows(2)
            heads_low(B - 2)
            residual(B - 2)
            divide(B - 1)
            cross_max(1)
            norm_rows(3)
            context_low(0)
            heads_low(B - 1)
            cross_reciprocal(1)
            residual(B - 1)
            cross_residual(0)
            cross_max(2)
            root_guess(1, 1)
            context_low(1)
            newton_step(1, 1, 0)
            cross_reciprocal(2)
            newton_step(1, 1, 1)
            newton_step(1, 1, 2)
            dve.wait_ge(root_ok, 10 * 2 * HALVES)
            norm_rows(4)
            cross_residual(1)
            for b in (3, 4):
                cross_max(b)
                if b == 3:
                    context_low(b - 1)
                norm_rows(b + 2)
                cross_reciprocal(b)
                if b > 3:
                    context_low(b - 1)
                cross_residual(b - 1)
            cross_max(5)
            root_guess(2, 0)
            norm_rows(7)
            cross_reciprocal(5)
            context_low(4)
            newton_step(2, 0, 0)
            newton_step(2, 0, 1)
            cross_residual(4)
            dve.wait_ge(xnp_ok, 4)
            cross_max(6)
            newton_step(2, 0, 2)
            ffn_norm(0)
            cross_reciprocal(6)
            ffn_norm(1)
            context_low(5)
            ffn_norm(2)
            cross_residual(5)
            ffn_norm(3)
            cross_max(7)
            ffn_in(0)
            cross_reciprocal(7)
            context_low(6)
            cross_residual(6)
            for f in range(2):
                ffn_hidden(0, f)
            context_low(7)
            cross_residual(7)
            root_guess(2, 1)
            newton_step(2, 1, 0)
            ffn_hidden(0, 3)
            newton_step(2, 1, 1)
            ffn_high(0, 6)
            ffn_hidden(0, 5)
            ffn_hidden(0, 6)
            ffn_hidden(0, 7)
            newton_step(2, 1, 2)
            ffn_norm(4)
            ffn_norm(5)
            ffn_norm(6)
            ffn_norm(7)
            ffn_in(1)
            for f in range(FB):
                if f == 2:
                    ffn_out(2)
                if f == 0:
                    ffn_out(0)
                    ffn_out(1)
                if by_vector(FB + f):
                    ffn_high(1, f)
                ffn_hidden(1, f)
            for b in range(HB - 1, B):
                ffn_out(b)

        @block.tensor
        def _(pe):
            def rows_to_columns(h, first, signal, to=(0, 1)):
                for k in range(KD):
                    for i in range(HB):
                        pe.wait_ge(xn_ok, first + HB * h + i + 1)
                        if first == 0:
                            after(pe, xnl_ok, KD * h)
                        mm = pe.transpose(banks[to[k]][:, S * i:S * i + S],
                                          xn_s[:, HB * h + i, P * k:P * k + P], eye_s[0:S, 0:S])
                    mm.then_inc(signal, 1)

            def split_over_k(out, lhs, rhs):
                for k in range(KD):
                    mm = pe.matmul(out, lhs(k), rhs(k), start=(k == 0), stop=(k == KD - 1))
                return mm

            def exact_product(out, left, right, late, late_low=None, late_high=None):
                products = ((0, 0), (1, 0), (0, 1)) if late == "right" else ((0, 0), (0, 1), (1, 0))
                for i, (a, b) in enumerate(products):
                    if i == 2 and late_low:
                        pe.wait_ge(*late_low)
                    for k in range(KD):
                        if i == 0 and late_high:
                            pe.wait_ge(late_high[0], late_high[1] + k)
                        mm = pe.matmul(out, left[a](k), right[b](k), start=(i == 0 and k == 0),
                                       stop=(i == 2 and k == KD - 1))
                return mm

            def both(high, low, a, b):
                return [lambda k: high[:, k, a:b], lambda k: low[:, k, a:b]]

            def query_key_block(n):
                h, m = n // 4, n % 4
                if h:
                    pe.wait_ge(*((r1_ok, n - 3) if m < 2 else (v_ok, n - 3)))
                pe.wait_ge(wh_ok, m + 1)
                pe.wait_ge(wl_ok, m + 1)
                exact_product(banks[QK_BANK[n % 4]][:, 0:HT], both(wh_s, wl_s, P * m, P * m + P),
                              both(xnh_t, xnl_t, HT * h, HT * h + HT), "right",
                              (xnl_ok, KD * (h + 1)), (xnt_ok, KD * h + 1)).then_inc(qkp_ok, 1)

            def value_rows(b):
                after(pe, v_ok, b - 3)
                if b % 4 >= 2:
                    pe.wait_ge(r1_ok, b + 1)
                pe.wait_ge(wh_ok, 5)
                pe.wait_ge(wl_ok, 5)
                exact_product(banks[V0 + b % 4][0:S, 0:D], both(xnh_t, xnl_t, S * b, S * b + S),
                              both(wh_s, wl_s, 2 * D, 3 * D), "left",
                              (xnl_ok, KD * (b // HB + 1))).then_inc(vp_ok, 1)

            def keep_warm(count):
                for _ in range(count):
                    pe.matmul(banks[AO][:, 0:HT], warm_s[:, 0:P], warm_s, start=True, stop=True)

            def clear_values_bank():
                pe.wait_ge(v_ok, B)
                pe.matmul(banks[OV][:, 0:NG * S], warm_s[:, 0:P], warm_s, start=True, stop=True).then_inc(ovz_ok, 1)

            pe.wait_ge(warm_ok, 1)
            keep_warm(WARM)
            pe.wait_ge(ld_eye, 16)
            rows_to_columns(0, 0, xnp_ok)
            for n in range(4):
                query_key_block(n)
            value_rows(0)
            value_rows(1)
            rows_to_columns(1, 0, xnp_ok)
            value_rows(2)
            value_rows(3)
            for n in range(4, 8):
                query_key_block(n)
            for b in range(HB, B):
                value_rows(b)

            def query_key_weights(m):
                split_over_k(banks[m][:, 0:D], lambda k: wq_s[:, k, P * m:P * m + P],
                             lambda k: wk_s[:, k, :]).then_inc(wa_p, 1)

            pe.wait_ge(xnl_ok, 2 * KD)
            pe.wait_ge(ld_wx, 64)
            for m in range(KD):
                query_key_weights(m)
            clear_values_bank()
            keep_warm(WARM_GAP)

            def masked_scores(bank, mask, left, right, toks, g, deep, signal):
                s = banks[bank][0:S, 0:GH * S]
                for i in range(GH):
                    pe.matmul(s[:, S * i:S * i + S], left[0:deep, GH * g + i, toks], right[0:deep, GH * g + i, toks],
                              start=(i == 0), stop=False)
                heads = s.rearrange("p (h s) -> p h s", h=GH)
                for a in (0, S - EDGE):
                    mm = pe.matmul(heads[:, :, a:a + EDGE], eyeb_s[0:S, 0:S],
                                   mask[:, a:a + EDGE].unsqueeze(1).to_broadcast([S, GH, EDGE]), start=False, stop=(a > 0))
                mm.then_inc(signal, 1)

            def scores(b, g):
                after(pe, max_ok, NG * b + g - (1 if b >= 2 else 3))
                masked_scores(score_bank(b, g), band_s, q_st, k_st, slice(S * b, S * b + S), g, QK, s_ok)

            def scores_t(b, g):
                if g == 0:
                    pe.wait_ge(shift_ld, 32 * (b + 1))
                after(pe, exp_ok, NG * b + g - 1)
                masked_scores(2 + g % 2, bandt_s, k_st, q_st, slice(S * b, S * b + S), g, QKM, st_p)

            def values(b, g):
                pe.wait_ge(exp_ok, NG * b + g + 1)
                if g == 0:
                    after(pe, ov_ok, b)
                for i in range(GH):
                    mm = pe.matmul(banks[OV][QUAD * i:QUAD * i + DH + 1, S * g:S * g + S], v_s[:, b, GH * g + i, :],
                                   pt_s[:, g % 2, i, :], start=True, stop=True)
                mm.then_inc(pv_ok, 1)

            def values_to_rows(b):
                pe.wait_ge(ov_ok, b + 1)
                after(pe, o_ok, b)
                for g in range(NG):
                    mm = pe.transpose(banks[OP][0:S, P * g:P * g + P], ov_s[:, g, :], eye_s[:])
                mm.then_inc(op_ok, 1)

            def heads_to_columns(b):
                pe.wait_ge(o_ok, b + 1)
                pe.wait_ge(sl_ok, min(B, b + 3))
                for k in range(KD):
                    mm = pe.transpose(banks[SMALL][:, S * k:S * k + S], o_s[:, P * k:P * k + P], eye_s[0:S, 0:S])
                mm.then_inc(otp_ok, 1)

            def max_to_columns(b):
                pe.wait_ge(max_ok, NG * b + NG)
                after(pe, sl_ok, b)
                after(pe, otl_ok, b - 2)
                pe.transpose(banks[SMALL][0:NH, 0:S], nmax[:, b % 2, :], eye_s[0:S, 0:S]).then_inc(mt_ok, 1)

            def project(b):
                pe.wait_ge(ot_ok, b + 1)
                after(pe, x1_ok, b)
                pe.wait_ge(wol_ok, 1)
                exact_product(banks[AO][0:S, 0:D], both(ot_h, ot_l, 0, S), both(wout_h, wout_l, 0, D), "left",
                              (otl_ok, b + 1)).then_inc(ao_ok, 1)

            def weight_sums():
                pe.wait_ge(ws_ok, 8)
                pe.wait_ge(ones_ok, 1)
                pe.wait_ge(x1_ok, 5)
                pe.matmul(banks[AO][:, 0:8], ones_s[:], wsum[:].rearrange("p a b -> p (a b)"),
                          start=True, stop=True).then_inc(wsp_ok, 1)

            def a_slot(b):
                for g in range(NG):
                    if b != 2 or g == 0:
                        scores(b, g)
                    if g == 0 and 1 <= b < 3:
                        max_to_columns(b - 1)
                    if b == 2 and g < NG - 1:
                        scores(b, g + 1)
                    if b >= 3:
                        if g == 1:
                            values_to_rows(b - 3)
                        if g == 2:
                            heads_to_columns(b - 3)
                    if b < 2:
                        keep_warm(1)
                    if 0 <= b - 2 < B:
                        scores_t(b - 2, g)
                        if g:
                            if b == 2 and g == 1:
                                pe.wait_ge(ovz_ok, 1)
                                pe.wait_ge(vones_ok, 1)
                            values(b - 2, g - 1)
                    if 0 <= b - 3 < B:
                        if g == 3:
                            project(b - 3)
                if 0 <= b - 2 < B:
                    values(b - 2, NG - 1)
                if b >= 2:
                    max_to_columns(b)

            def norm_to_columns(b):
                pe.wait_ge(xr_ok, b + 1)
                after(pe, tt_ok, b)
                for k in range(KD):
                    mm = pe.transpose(banks[XT][:, S * k:S * k + S], xr_s[:, P * k:P * k + P], eye_s[0:S, 0:S])
                mm.then_inc(xtp_ok, 1)

            def queries(b):
                pe.wait_ge(xt_ok, b + 1)
                for m in range(KD):
                    mm = split_over_k(banks[TT][:, S * (KD + m):S * (KD + m + 1)], lambda k: wa_s[:, k, P * m:P * m + P],
                                      lambda k: xt_s[:, k, :])
                mm.then_inc(ttp_ok, 1)

            def cross_scores(b):
                pe.wait_ge(tt_ok, b + 1)
                pe.wait_ge(ld_ctxt[b // 2], 16)
                after(pe, sc_ok, b)
                split_over_k(banks[SC][0:S, 0:S2], lambda k: tt_s[:, k, :],
                             lambda k: ctx_t[:, k, S2 * b:S2 * b + S2]).then_inc(s2_ok, 1)

            def probs_to_columns(b):
                pe.wait_ge(e2_ok, b + 1)
                after(pe, pt_ok, b)
                for c in range(CC):
                    mm = pe.transpose(banks[PT][0:CP, S * c:S * c + S], p2_s[:, CP * c:CP * c + CP], eye_s[0:S, 0:S])
                mm.then_inc(ptp_ok, 1)

            def weighted_context(b):
                pe.wait_ge(pt_ok, b + 1)
                pe.wait_ge(ld_ctxr[b // 2], 16)
                after(pe, ytl_ok, b)
                for m in range(KD):
                    for c in range(CC):
                        mm = pe.matmul(banks[YY][:, S * m:S * m + S], ctx_r[:, b * CC + c, P * m:P * m + P],
                                       p2t_s[:, c, :], start=(c == 0), stop=(c == CC - 1))
                mm.then_inc(yp_ok, 1)

            def cross_project(b):
                pe.wait_ge(yt_ok, b + 1)
                after(pe, x2_ok, b)
                pe.wait_ge(wol_ok, 2)
                exact_product(banks[CO][0:S, 0:D], both(yt_h, yt_l, 0, S), both(wvt_h, wvt_l, 0, D), "left",
                              (ytl_ok, b + 1)).then_inc(co_ok, 1)

            def x_slot(b):
                if 0 <= b - 1 < B:
                    probs_to_columns(b - 1)
                if b < B:
                    cross_scores(b)
                if b + 1 < B:
                    norm_to_columns(b + 1)
                if 0 <= b - 1 < B:
                    weighted_context(b - 1)
                if b + 1 < B:
                    queries(b + 1)
                if 0 <= b - 1 < B:
                    cross_project(b - 1)

            def ffn_in(h):
                after(pe, h_ok, FB * h)
                rows_to_columns(h, B, x3p_ok, HID)

            def ffn_hidden(h, f):
                n = FB * h + f
                if f < KD:
                    pe.wait_ge(x3l_ok, KD * h + f + 1)
                elif h and f == KD:
                    pe.wait_ge(x2_ok, B)
                else:
                    after(pe, h_ok, n - 1 - h)
                for j, (part, done) in enumerate(((xh_t, x3h_ok), (xl_t, x3l_ok))):
                    for k in range(KD):
                        if f == 0:
                            pe.wait_ge(done, KD * h + k + 1)
                        mm = pe.matmul(banks[HIDDEN_BANK[n]][:, 0:HT], w1_r[:, k, P * f:P * f + P],
                                       part[:, k, HT * h:HT * h + HT], start=(k == 0 and j == 0),
                                       stop=(k == KD - 1 and j == 1))
                mm.then_inc(hp_ok, 1)

            def ffn_out(b):
                after(pe, y2_ok, b - 3)
                parts = [(f, 0) for f in range(FB - 1)] + [(f, 1) for f in range(FB - 2)]
                parts += [(FB - 1, 0), (FB - 2, 1), (FB - 1, 1)]
                for i, (f, low) in enumerate(parts):
                    if low:
                        wait_low(pe, FB * (b // HB) + f)
                    else:
                        wait_high(pe, FB * (b // HB) + f)
                    mm = pe.matmul(banks[OUT[b % 4]][0:S, 0:D], (hl_s if low else hh_s)[:, f, S * b:S * b + S],
                                   w2_r[:, f, :], start=(i == 0), stop=(i == 2 * FB - 1))
                mm.then_inc(f_ok, 1)

            pe.wait_ge(ld_c, 16 * 7)
            pe.wait_ge(kones_ok, 16)
            pe.wait_ge(wa_ok, KD)
            pe.wait_ge(r1_ok, 8)
            for b in range(B):
                if b % HB == 0:
                    pe.wait_ge(qk_ld[b // HB], 16 * (len(Q_RUNS) + len(K_RUNS)))
                a_slot(b)
            scores_t(B - 2, 0)
            scores_t(B - 2, 1)
            values_to_rows(B - 3)
            values(B - 2, 0)
            weight_sums()
            scores_t(B - 2, 2)
            values(B - 2, 1)
            heads_to_columns(B - 3)
            norm_to_columns(0)
            scores_t(B - 2, 3)
            values(B - 2, 2)
            pe.wait_ge(thr_sum, 1)
            project(B - 3)
            queries(0)
            values(B - 2, 3)
            scores_t(B - 1, 0)
            scores_t(B - 1, 1)
            values_to_rows(B - 2)
            cross_scores(0)
            values(B - 1, 0)
            norm_to_columns(1)
            heads_to_columns(B - 2)
            scores_t(B - 1, 2)
            values(B - 1, 1)
            queries(1)
            scores_t(B - 1, 3)
            values(B - 1, 2)
            project(B - 2)
            values(B - 1, 3)
            probs_to_columns(0)
            cross_scores(1)
            values_to_rows(B - 1)
            norm_to_columns(2)
            weighted_context(0)
            heads_to_columns(B - 1)
            queries(2)
            cross_project(0)
            project(B - 1)
            for b in range(2, B - 1):
                x_slot(b)
            pe.wait_ge(otl_ok, B)
            pe.wait_ge(x1_ok, B)
            probs_to_columns(B - 2)
            cross_scores(B - 1)
            ffn_in(0)
            weighted_context(B - 2)
            pe.wait_ge(tern_ok, KD * F // TC)
            ffn_hidden(0, 0)
            cross_project(B - 2)
            ffn_hidden(0, 1)
            probs_to_columns(B - 1)
            ffn_hidden(0, 2)
            weighted_context(B - 1)
            ffn_hidden(0, 3)
            cross_project(B - 1)
            for f in range(4, FB):
                ffn_hidden(0, f)
            pe.wait_ge(tern_ok, 2 * KD * F // TC)
            pe.wait_ge(tt_ok, B)
            pe.wait_ge(sc_ok, B)
            pe.wait_ge(pt_ok, B)
            ffn_out(0)
            ffn_out(1)
            ffn_in(1)
            ffn_out(2)
            ffn_hidden(1, 0)
            ffn_hidden(1, 1)
            for f in range(2, FB):
                ffn_hidden(1, f)
            for b in range(HB - 1, B):
                ffn_out(b)


def kernel(**inputs):
    import numpy as np
    import concourse.bacc as bacc
    from concourse.bass_utils import run_bass_kernel_spmd as run

    def rows(a):
        return np.ascontiguousarray(a)

    order = np.array([side * D + (2 * g + k) * DH + d
                      for side in range(2) for k in range(2) for d in range(DH) for g in range(NH // 2)])
    w_qkv = np.asarray(inputs["L0_attn_w_qkv"])
    b_qkv = np.asarray(inputs["L0_attn_b_qkv"])
    i, j = np.arange(S)[:, None], np.arange(S)[None, :]
    allowed = (j % STRIDE == 0) | (np.abs(i - j) <= WINDOW)
    bf16 = mybir.dt.np(BF16)
    band = np.where(allowed, 0.0, BIG).astype(bf16)
    ctx = np.asarray(inputs["ctx_1024"]).reshape(B * S2, D)
    arrays = {
        "x": rows(inputs["x"]),
        "ctx_rows": rows(ctx),
        "ctx_cols": rows(ctx.T),
        "mask": rows(inputs["mask_SxS2_ik0"]),
        "w_qkv": rows(np.concatenate([w_qkv[:, order], w_qkv[:, 2 * D:]], axis=1)),
        "b_qk": rows(b_qkv[order].reshape(4, P).T),
        "b_v": rows(b_qkv[2 * D:]),
        "w_out": rows(inputs["L0_attn_w_out"]),
        "b_out": rows(inputs["L0_attn_b_out"]),
        "wq": rows(inputs["L0_xattn_Wq"]),
        "wk": rows(inputs["L0_xattn_Wk"]),
        "wv_t": rows(np.asarray(inputs["L0_xattn_Wv"]).T),
        "w1_t": rows(np.asarray(inputs["L0_ffn_W1"]).T),
        "b1": rows(np.asarray(inputs["L0_ffn_b1"]).reshape(FB, P).T),
        "w2_t": rows(np.asarray(inputs["L0_ffn_W2"]).T),
        "b2": rows(inputs["L0_ffn_b2"]),
        "eye": np.eye(P, dtype=np.float32),
        "eye_b": np.eye(P).astype(bf16),
        "k_ones": np.ones((QKM - QK, NH * T), dtype=bf16),
        "band": band,
        "band_t": rows(band.T),
    }
    nc = bacc.Bacc("TRN2", target_bir_lowering=False, num_devices=1)
    aps = {name: nc.dram_tensor(name, a.shape, mybir.dt.from_np(a.dtype), kind="ExternalInput").ap()
           for name, a in arrays.items()}
    out = nc.dram_tensor("out", (B, S, D), F32, kind="ExternalOutput").ap()
    build(nc, out=out, **aps)
    return run(nc, [arrays], core_ids=[0]).results[0]["out"]
```
